# Optimizing a Trainium2 kernel written in Bass

```python
import numpy as np
import jax
import jax.numpy as jnp

def _softmax(x, axis=-1):
    return jax.nn.softmax(x, axis=axis)

def _gelu(x):
    return jax.nn.gelu(x, approximate=True)

def _silu(x):
    return jax.nn.silu(x)

def _sigmoid(x):
    return jax.nn.sigmoid(x)

def _layernorm(x, axis=-1, eps=1e-05):
    m = jnp.mean(x, axis=axis, keepdims=True)
    v = jnp.var(x, axis=axis, keepdims=True)
    return (x - m) / jnp.sqrt(v + eps)

def _scatter_add(tgt, idx, src, axis=0):
    return tgt.at[idx].add(src)

def _segment_sum(src, seg, n):
    return jax.ops.segment_sum(src, seg, n)
kernel_name = 'mk_cond_resid_d2_seqx_r4_6558fc'

def setup_inputs(seed: int=0):
    np.random.seed(seed)
    _w = jnp.asarray

    def _rec_inputs():
        import jax
        import jax.numpy as jnp
        _rk = jax.random.key(seed)
        x = -0.0003929 + 0.9999 * jax.random.normal(jax.random.fold_in(_rk, 1), (2, 1024, 256), jnp.float32)
        _lenS = 1024 - jax.random.randint(jax.random.fold_in(_rk, 7), (2,), 0, max(1, 1024 // 4) + 1, jnp.int32)
        _lenS2 = 1024 - jax.random.randint(jax.random.fold_in(_rk, 8), (2,), 0, max(1, 1024 // 4) + 1, jnp.int32)
        cond_256 = -0.0209273 + 1.04763 * jax.random.normal(jax.random.fold_in(_rk, 11), (2, 64), jnp.float32)
        return (x, cond_256)
    x, cond_256 = _rec_inputs()

    def _L0_cond_setup():
        import jax, jax.numpy as jnp
        import numpy as np
        EPS = 1e-08

        def hamilton(q1, q2):
            w1, x1, y1, z1 = (q1[..., i, :] for i in range(4))
            w2, x2, y2, z2 = (q2[..., i, :] for i in range(4))
            w = w1 * w2 - x1 * x2 - y1 * y2 - z1 * z2
            x = w1 * x2 + x1 * w2 + y1 * z2 - z1 * y2
            y = w1 * y2 - x1 * z2 + y1 * w2 + z1 * x2
            z = w1 * z2 + x1 * y2 - y1 * x2 + z1 * w2
            return jnp.stack([w, x, y, z], axis=-2)

        def _normalize(q):
            return q / jnp.sqrt(jnp.sum(q * q, axis=0, keepdims=True) + EPS)
        key = jax.random.key(seed)
        k1, k2, k3, k4 = jax.random.split(key, 4)
        B, T, d_model = (4, 1024, 256)
        quat_dim = d_model // 4
        x = jax.random.normal(k1, (B, T, d_model), dtype=jnp.float32)
        q_left = jax.random.normal(k2, (4, quat_dim), dtype=jnp.float32)
        q_right = jax.random.normal(k3, (4, quat_dim), dtype=jnp.float32)
        spectral_gate = jax.random.uniform(k4, (1, 1, 1, quat_dim), dtype=jnp.float32)
        return {'x': x, 'q_left': q_left, 'q_right': q_right, 'spectral_gate': spectral_gate}
    _L0_cond_all = _L0_cond_setup()
    _L0_cond_in = {k: v for k, v in _L0_cond_all.items() if k in ('q_right', 'spectral_gate')}
    del _L0_cond_all

    def _L1_cond_setup():
        import jax, jax.numpy as jnp
        import numpy as np
        D_MODEL = 256
        D_T = 64
        N_HEADS = 16
        HIDDEN = 4 * D_MODEL
        EPS = 1e-06

        def _tc_rmsnorm(x, t, gw, gb, bw, bb):
            g = (t @ gw.T + gb)[:, None, :]
            b = (t @ bw.T + bb)[:, None, :]
            inv_rms = jax.lax.rsqrt(jnp.mean(x * x, axis=-1, keepdims=True) + EPS)
            return g * x * inv_rms + b

        def _attention(x, Wq, Wk, Wv, Wo):
            B, L, D = x.shape
            H = N_HEADS
            dh = D // H
            scale = np.sqrt(dh).astype(np.float32)
            q = (x @ Wq.T).reshape(B, L, H, dh)
            k = (x @ Wk.T).reshape(B, L, H, dh)
            v = (x @ Wv.T).reshape(B, L, H, dh)
            attn = jnp.einsum('blhd,bmhd->bhlm', q, k) / scale
            p = jax.nn.softmax(attn, axis=-1)
            o = jnp.einsum('bhlm,bmhd->blhd', p, v).reshape(B, L, D)
            return o @ Wo.T

        def _swiglu(x, gate_w, hid_w, out_w):
            return jax.nn.silu(x @ gate_w.T) * (x @ hid_w.T) @ out_w.T
        key = jax.random.key(seed)
        ks = jax.random.split(key, 20)
        B, L = (8, 256)
        s_d = 1.0 / np.sqrt(D_MODEL)
        s_t = 1.0 / np.sqrt(D_T)
        s_h = 1.0 / np.sqrt(HIDDEN)
        return {'x': jax.random.normal(ks[0], (B, L, D_MODEL), jnp.float32), 't': jax.random.normal(ks[1], (B, D_T), jnp.float32), 'Wq': jax.random.normal(ks[2], (D_MODEL, D_MODEL), jnp.float32) * s_d, 'Wk': jax.random.normal(ks[3], (D_MODEL, D_MODEL), jnp.float32) * s_d, 'Wv': jax.random.normal(ks[4], (D_MODEL, D_MODEL), jnp.float32) * s_d, 'Wo': jax.random.normal(ks[5], (D_MODEL, D_MODEL), jnp.float32) * s_d, 'g1w': jax.random.normal(ks[6], (D_MODEL, D_T), jnp.float32) * s_t, 'g1b': jnp.ones((D_MODEL,), jnp.float32), 'b1w': jax.random.normal(ks[7], (D_MODEL, D_T), jnp.float32) * s_t, 'b1b': jnp.zeros((D_MODEL,), jnp.float32), 'g2w': jax.random.normal(ks[8], (D_MODEL, D_T), jnp.float32) * s_t, 'g2b': jnp.ones((D_MODEL,), jnp.float32), 'b2w': jax.random.normal(ks[9], (D_MODEL, D_T), jnp.float32) * s_t, 'b2b': jnp.zeros((D_MODEL,), jnp.float32), 'gate_w': jax.random.normal(ks[10], (HIDDEN, D_MODEL), jnp.float32) * s_d, 'hid_w': jax.random.normal(ks[11], (HIDDEN, D_MODEL), jnp.float32) * s_d, 'out_w': jax.random.normal(ks[12], (D_MODEL, HIDDEN), jnp.float32) * s_h}
    _L1_cond_all = _L1_cond_setup()
    _L1_cond_in = {k: v for k, v in _L1_cond_all.items() if k in ('Wq', 'Wk', 'Wv', 'Wo', 'g1w', 'g1b', 'b1w', 'b1b', 'g2w', 'g2b', 'b2w', 'b2b', 'gate_w', 'hid_w', 'out_w')}
    del _L1_cond_all
    return {'x': x, 'cond_256': cond_256, 'L0_cond_q_right': _L0_cond_in['q_right'], 'L0_cond_spectral_gate': _L0_cond_in['spectral_gate'], 'L1_cond_Wq': _L1_cond_in['Wq'], 'L1_cond_Wk': _L1_cond_in['Wk'], 'L1_cond_Wv': _L1_cond_in['Wv'], 'L1_cond_Wo': _L1_cond_in['Wo'], 'L1_cond_g1w': _L1_cond_in['g1w'], 'L1_cond_g1b': _L1_cond_in['g1b'], 'L1_cond_b1w': _L1_cond_in['b1w'], 'L1_cond_b1b': _L1_cond_in['b1b'], 'L1_cond_g2w': _L1_cond_in['g2w'], 'L1_cond_g2b': _L1_cond_in['g2b'], 'L1_cond_b2w': _L1_cond_in['b2w'], 'L1_cond_b2b': _L1_cond_in['b2b'], 'L1_cond_gate_w': _L1_cond_in['gate_w'], 'L1_cond_hid_w': _L1_cond_in['hid_w'], 'L1_cond_out_w': _L1_cond_in['out_w']}

def reference(x, cond_256, L0_cond_q_right, L0_cond_spectral_gate, L1_cond_Wq, L1_cond_Wk, L1_cond_Wv, L1_cond_Wo, L1_cond_g1w, L1_cond_g1b, L1_cond_b1w, L1_cond_b1b, L1_cond_g2w, L1_cond_g2b, L1_cond_b2w, L1_cond_b2b, L1_cond_gate_w, L1_cond_hid_w, L1_cond_out_w):
    import jax
    import jax.numpy as jnp

    def _L0_cond_ref(x, q_left, q_right, spectral_gate):
        import jax, jax.numpy as jnp
        import numpy as np
        EPS = 1e-08

        def hamilton(q1, q2):
            w1, x1, y1, z1 = (q1[..., i, :] for i in range(4))
            w2, x2, y2, z2 = (q2[..., i, :] for i in range(4))
            w = w1 * w2 - x1 * x2 - y1 * y2 - z1 * z2
            x = w1 * x2 + x1 * w2 + y1 * z2 - z1 * y2
            y = w1 * y2 - x1 * z2 + y1 * w2 + z1 * x2
            z = w1 * z2 + x1 * y2 - y1 * x2 + z1 * w2
            return jnp.stack([w, x, y, z], axis=-2)

        def _normalize(q):
            return q / jnp.sqrt(jnp.sum(q * q, axis=0, keepdims=True) + EPS)
        B, T, d_model = x.shape
        quat_dim = d_model // 4
        x_quat = x.reshape(B, T, 4, quat_dim)
        x_spectral = jnp.fft.fft(x_quat, axis=1)
        x_filtered = jnp.fft.ifft(x_spectral * spectral_gate, axis=1).real.astype(x.dtype)
        q_left_n = _normalize(q_left)
        q_right_n = _normalize(q_right)
        conj_sign = jnp.array([1.0, -1.0, -1.0, -1.0], dtype=x.dtype)[:, None]
        q_right_conj = q_right_n * conj_sign
        x_right = hamilton(x_filtered, q_right_conj)
        x_rotated = hamilton(q_left_n, x_right)
        return x_rotated.reshape(B, T, d_model)

    def _L1_cond_ref(x, t, Wq, Wk, Wv, Wo, g1w, g1b, b1w, b1b, g2w, g2b, b2w, b2b, gate_w, hid_w, out_w):
        import jax, jax.numpy as jnp
        import numpy as np
        D_MODEL = 256
        D_T = 64
        N_HEADS = 16
        HIDDEN = 4 * D_MODEL
        EPS = 1e-06

        def _tc_rmsnorm(x, t, gw, gb, bw, bb):
            g = (t @ gw.T + gb)[:, None, :]
            b = (t @ bw.T + bb)[:, None, :]
            inv_rms = jax.lax.rsqrt(jnp.mean(x * x, axis=-1, keepdims=True) + EPS)
            return g * x * inv_rms + b

        def _attention(x, Wq, Wk, Wv, Wo):
            B, L, D = x.shape
            H = N_HEADS
            dh = D // H
            scale = np.sqrt(dh).astype(np.float32)
            q = (x @ Wq.T).reshape(B, L, H, dh)
            k = (x @ Wk.T).reshape(B, L, H, dh)
            v = (x @ Wv.T).reshape(B, L, H, dh)
            attn = jnp.einsum('blhd,bmhd->bhlm', q, k) / scale
            p = jax.nn.softmax(attn, axis=-1)
            o = jnp.einsum('bhlm,bmhd->blhd', p, v).reshape(B, L, D)
            return o @ Wo.T

        def _swiglu(x, gate_w, hid_w, out_w):
            return jax.nn.silu(x @ gate_w.T) * (x @ hid_w.T) @ out_w.T
        x = x + _attention(_tc_rmsnorm(x, t, g1w, g1b, b1w, b1b), Wq, Wk, Wv, Wo)
        return x + _swiglu(_tc_rmsnorm(x, t, g2w, g2b, b2w, b2b), gate_w, hid_w, out_w)
    x = x + _L0_cond_ref(x, cond_256, L0_cond_q_right, L0_cond_spectral_gate)
    x = x + _L1_cond_ref(x, cond_256, L1_cond_Wq, L1_cond_Wk, L1_cond_Wv, L1_cond_Wo, L1_cond_g1w, L1_cond_g1b, L1_cond_b1w, L1_cond_b1b, L1_cond_g2w, L1_cond_g2b, L1_cond_b2w, L1_cond_b2b, L1_cond_gate_w, L1_cond_hid_w, L1_cond_out_w)
    return x

_drawn_inputs = setup_inputs


def setup_inputs(seed=0):
    import zlib

    import numpy as np

    out = dict(_drawn_inputs(seed))
    spreads = {'L1_cond_g1b': (1.0, 0.2),
     'L1_cond_b1b': (0.0, 0.1),
     'L1_cond_g2b': (1.0, 0.2),
     'L1_cond_b2b': (0.0, 0.1)}
    factors = {}
    for name, (base, spread) in spreads.items():
        noise = np.random.default_rng([zlib.crc32(name.encode()), seed]).standard_normal(out[name].shape)
        drawn = base * np.exp(spread * noise) if base else spread * noise
        out[name] = jnp.asarray(drawn.astype(out[name].dtype))
    for name, factor in factors.items():
        out[name] = (out[name] * factor).astype(out[name].dtype)
    return out
```

```python
import concourse.bass as bass
from concourse import mybir
from contextlib import ExitStack

P = 128
BATCH, SEQ, D = 2, 1024, 256
HEADS, DH = 16, 16
HIDDEN = 1024
QUAT = D // 4
DT = 64
TOK = BATCH * SEQ
NT = TOK // P
CT = 4
CW = CT * P
NCH = NT // CT
BCH = NCH // BATCH
KT = D // P
GH = 4
NG = BATCH * HEADS // GH
LT = SEQ // P
HALF = 512
NHALF = SEQ // HALF
VW = DH + 1
Q_PARTS = ((0, 3), (1, 2), (2, 1))
K_PARTS = (0, 1, 2, 0, 1, 0)
PROD_ROWS = DH * len(K_PARTS)
ALL_ROWS = PROD_ROWS + 3
SLOTS = 3
EB = 3
PR = 8
LEAD = 8
HT = HIDDEN // P
QEPS, NEPS = 1e-8, 1e-6


def build(nc, x, cond, q_right, gate, wq, wk, wv, wo, g1w, g1b, b1w, b1b, g2w, g2b, b2w, b2b,
          gate_w, hid_w, out_w, out):
    f32, f32r, bf16 = mybir.dt.float32, mybir.dt.float32r, mybir.dt.bfloat16
    ALU, ACT, AX = mybir.AluOpType, mybir.ActivationFunctionType, mybir.AxisListType

    ctx = ExitStack()
    with ctx:
        def sb(name, shape, dt, scope=None):
            return (scope or ctx).enter_context(nc.sbuf_tensor(name, shape, dt))

        def sem(name):
            return ctx.enter_context(nc.semaphore(name))

        ident = sb("ident", [P, P], f32)
        ident_bf = sb("ident_bf", [P, P], bf16)
        x1 = sb("x1", [P, NT, D], f32)
        attn = sb("attn", [P, NT, D], f32)
        wo_hi, wo_lo = (sb(f"wo_{s}", [P, KT, D], f32r) for s in ("hi", "lo"))
        gb = sb("gb", [P, BATCH, 8], f32)
        sumsq = sb("sumsq", [P, 2, NT], f32)
        rms = sb("rms", [P, 2, NT], f32)
        inv_rms = sb("inv_rms", [P, 2, NT], f32)
        qc = sb("qc", [P, 15], f32)
        squares = sb("squares", [P, 2, D], f32)

        scope_b = ExitStack()
        v_sb = sb("v_sb", [P, NT, HEADS, VW], f32, scope_b)
        q_st = [sb(f"q_st{i}", [P, GH, SEQ], bf16, scope_b) for i in range(SLOTS)]
        k_st = [sb(f"k_st{i}", [P, GH, SEQ], bf16, scope_b) for i in range(SLOTS)]

        scope_p = ExitStack()
        par_rows = sb("par_rows", [15, P], f32, scope_p)
        cond_bc = sb("cond_bc", [P, BATCH, DT], f32, scope_p)
        gw = sb("gw", [P, 8, DT], f32, scope_p)
        gprod = sb("gprod", [P, 8, DT], f32, scope_p)
        diag64 = sb("diag64", [P, QUAT], f32, scope_p)
        small = sb("small", [P, 64], f32, scope_p)
        rot = sb("rot", [P, KT, D], f32, scope_p)
        w_raw = sb("w_raw", [P, 4, KT, D], f32, scope_p)
        w_hi = sb("w_hi", [P, 3, KT, D], f32r, scope_p)
        w_lo = sb("w_lo", [P, 3, KT, D], f32r, scope_p)
        x_in = [sb(f"x_in{i}", [P, CT, D], f32, scope_p) for i in range(2)]
        x_t = [sb(f"x_t{i}", [P, KT, CW], f32, scope_p) for i in range(2)]
        xs = [sb(f"xs{i}", [P, CT, D], f32, scope_p) for i in range(2)]
        xf = sb("xf", [P, KT, CW], f32, scope_p)
        xn_hi = [sb(f"xn_hi{i}", [P, KT, CW], f32r, scope_p) for i in range(2)]
        xn_lo = [sb(f"xn_lo{i}", [P, KT, CW], f32r, scope_p) for i in range(2)]
        qk_rest = [sb(f"qk_rest{i}", [P, CW], f32, scope_p) for i in range(2)]
        qk_parts = [sb(f"qk_parts{i}", [P, 3, CW], bf16, scope_p) for i in range(4)]
        scope_p.close()

        prob = [sb(f"prob{i}", [P, HALF], f32, scope_b) for i in range(PR)]
        ot = [sb(f"ot{i}", [P, HALF], f32, scope_b) for i in range(2)]
        nmax = sb("nmax", [P, 2, GH, LT], f32, scope_b)
        nmax_rest = sb("nmax_rest", [P, GH * LT], f32, scope_b)
        nmax_parts = sb("nmax_parts", [P, 3, GH * LT], bf16, scope_b)
        nmax_t = sb("nmax_t", [3 * GH * LT, P], bf16, scope_b)
        rsum = sb("rsum", [P, CT, GH, 1], f32, scope_b)
        f_raw = sb("f_raw", [P, 3, 8, D], f32, scope_b)
        fw_hi = sb("fw_hi", [P, 2, KT, HIDDEN], f32r, scope_b)
        fw_lo = sb("fw_lo", [P, 2, KT, HIDDEN], f32r, scope_b)
        fo_hi = sb("fo_hi", [P, HT, D], f32r, scope_b)
        fo_lo = sb("fo_lo", [P, HT, D], f32r, scope_b)
        silu_g = [sb(f"silu_g{i}", [P, CW], f32, scope_b) for i in range(2)]
        h_f = [sb(f"h_f{i}", [P, CW], f32, scope_b) for i in range(2)]
        scope_b.close()
        h_hi = [sb(f"h_hi{i}", [P, CW], f32r) for i in range(3)]
        h_lo = [sb(f"h_lo{i}", [P, CW], f32r) for i in range(3)]
        at_hi = sb("at_hi", [P, KT, CW], f32r)
        at_lo = sb("at_lo", [P, KT, CW], f32r)
        xs2 = sb("xs2", [P, CT, D], f32)
        yn_f = sb("yn_f", [P, KT, CW], f32)
        yn_hi = [sb(f"yn_hi{i}", [P, KT, CW], f32r) for i in range(NCH)]
        yn_lo = [sb(f"yn_lo{i}", [P, KT, CW], f32r) for i in range(NCH)]

        psum = ctx.enter_context(nc.psum_tensor("psum", [P, 8, 512], f32))
        scr_qk = nc.dram_tensor("scr_qk", (2, 3, D, TOK), bf16, kind="Internal").ap()
        scr_max = nc.dram_tensor("scr_max", (NG, 3, GH * SEQ), bf16, kind="Internal").ap()

        plan, bank_total = {}, [0] * 8
        before = {}

        def plan_tile(key, bank):
            before[key] = bank_total[bank]
            bank_total[bank] += 1
            plan[key] = (len(plan), bank, bank_total[bank])

        ring = [0]

        def plan_ring(key):
            plan_tile(key, ring[0] % 8)
            ring[0] += 1

        prep_steps = [("x_T", 0), ("W", 0), ("L0", 0), ("x_T", 1), ("L0", 1), ("xs_T", 0),
                      ("x_T", 2), ("L0", 2), ("QKV", 0), ("xs_T", 1),
                      ("x_T", 3), ("L0", 3), ("QKV", 1), ("xs_T", 2), ("QKV", 2), ("xs_T", 3), ("QKV", 3)]
        plan_ring(("par",))
        for what, c in prep_steps:
            if what == "W":
                for i in range(4):
                    plan_ring(("w", i))
            elif what == "QKV":
                for j in range(4):
                    plan_ring(("qk", c, j))
                for pair in range(2):
                    plan_ring(("v", c, pair))
            else:
                for i in range(2):
                    plan_ring((what, c, i))
        prep_total = list(bank_total)
        fin_steps = [("a_T", 0), ("WO", 0), ("FW", 0), ("a_T", 1), ("WO", 1), ("y_T", 0), ("FW", 1),
                     ("a_T", 2), ("WO", 2), ("y_T", 1), ("FW", 2), ("a_T", 3), ("WO", 3), ("y_T", 2),
                     ("FW", 3), ("y_T", 3)]
        for what, c in fin_steps:
            if what == "FW":
                for i in range(3):
                    plan_ring(("fw", 3 * c + i))
            else:
                for i in range(2):
                    plan_ring((what, c, i))
        ffn_units = [(c, ht) for c in range(NCH) for ht in range(HT)]
        OUT_LAG = 2
        for n in range(len(ffn_units) + OUT_LAG):
            if n < len(ffn_units):
                plan_tile(("gate", n), 4 + (2 * n) % 4)
                plan_tile(("hid", n), 4 + (2 * n + 1) % 4)
            if n >= OUT_LAG and ffn_units[n - OUT_LAG][1] == HT - 1:
                for tt in range(CT):
                    plan_tile(("out", ffn_units[n - OUT_LAG][0], tt), tt)

        NSTEP = NG * NHALF * LT
        UNITS = NG * GH * LT
        GU = GH * LT

        def max_items(step):
            if step < 0:
                return ([("max", u) for u in range(GU)] + [("max", u) for u in range(GU, GU + 2)] + [("T", 0)]
                        + [("max", u) for u in range(GU + 2, GU + LEAD)])
            items = []
            if step % LT == 1 and step > LT:
                items.append(("O", step // LT - 1))
            first = GU + LEAD + 2 * step
            if first % GU == 2:
                items += [("T", first // GU - 1)] if first // GU - 1 < NG else []
            items += [("max", u) for u in (first, first + 1) if u < UNITS]
            return items

        max_no = {}
        for step in range(-1, NSTEP + 2):
            for item in max_items(step):
                max_no[item] = len(max_no)
        assert all(("T", g) in max_no for g in range(NG)) and ("O", NG * NHALF - 1) in max_no

        par_loaded = sem("par_loaded")
        cond_loaded = sem("cond_loaded")
        w_loaded = sem("w_loaded")
        x_loaded = [sem(f"x_loaded{c}") for c in range(NCH)]
        f_loaded = sem("f_loaded")
        consts_ready = sem("consts_ready")
        tile_filled = sem("tile_filled")
        evacuated = [sem(f"evacuated{i}") for i in range(8)]
        vector_step = sem("vector_step")
        pool_step = sem("pool_step")
        norms_summed = sem("norms_summed")
        norms_rooted = sem("norms_rooted")
        rot_ready = sem("rot_ready")
        gb_ready = sem("gb_ready")
        w_hi_ready = sem("w_hi_ready")
        ms_ready = sem("ms_ready")
        rms_ready = sem("rms_ready")
        xs_ready = sem("xs_ready")
        xn_hi_ready = sem("xn_hi_ready")
        xn_lo_ready = sem("xn_lo_ready")
        part1_ready = sem("part1_ready")
        parts_ready = sem("parts_ready")
        parts_saved = [sem(f"parts_saved{j}") for j in range(4)]
        stack_loaded = [sem(f"stack_loaded{i}") for i in range(SLOTS)]
        max_loaded = [sem(f"max_loaded{i}") for i in range(SLOTS)]
        nmax_saved = sem("nmax_saved")
        max_filled = sem("max_filled")
        max_used = sem("max_used")
        nmax_split = sem("nmax_split")
        o_cleared = sem("o_cleared")
        scores_filled = sem("scores_filled")
        exp_done = sem("exp_done")
        pv_done = sem("pv_done")
        o_copied = sem("o_copied")
        at_hi_ready = sem("at_hi_ready")
        squares_done = sem("squares_done")
        x12_ready = sem("x12_ready")
        ys_ready = sem("ys_ready")
        yn_hi_ready = sem("yn_hi_ready")
        yn_lo_ready = sem("yn_lo_ready")
        fw_hi_ready = sem("fw_hi_ready")
        h_hi_ready = sem("h_hi_ready")
        h_lo_ready = sem("h_lo_ready")
        h_used = sem("h_used")
        stored = sem("stored")

        def wait_filled(eng, *key):
            eng.wait_ge(tile_filled, plan[key][0] + 1)

        def wait_evacuated(eng, *key):
            eng.wait_ge(evacuated[plan[key][1]], plan[key][2])

        def wait_bank(eng, *key):
            if before[key]:
                eng.wait_ge(evacuated[plan[key][1]], before[key])

        def bank_of(*key):
            return psum[:, plan[key][1], :]

        def free_sem(*key):
            return evacuated[plan[key][1]]

        def max_slot(item):
            s = 2 * (max_no[item] % 2)
            return psum[:, s:s + 2, :]

        def e_bank(e):
            return psum[:, 4 + e % EB, :]

        O_BANK = psum[:, 7, :]
        def gb_col(b, norm, off, kt):
            i = 4 * norm + 2 * off + kt
            return gb[:, b, i:i + 1]

        def wait_h_used(eng, n):
            c, ht = ffn_units[n]
            if ht == HT - 1:
                wait_filled(eng, "out", c, CT - 1)
            else:
                eng.wait_ge(h_used, c * (HT - 1) + ht + 1)

        def fw_src(n):
            if n < 8:
                return bank_of("fw", n)
            return bank_of("fw", n).rearrange("p (a d) -> p a d", a=2)

        def fw_dst(n, part):
            if n < 8:
                w, kt, half = n // 4, n // 2 % 2, n % 2
                return (fw_hi, fw_lo)[part][:, w, kt, half * 512:half * 512 + 512]
            ht = 2 * (n - 8)
            return (fo_hi, fo_lo)[part][:, ht:ht + 2, :]

        block = ctx.enter_context(nc.Block())

        @block.sync
        def _(sp):
            for half in range(2):
                cols = slice(half * QUAT, (half + 1) * QUAT)
                sp.dma_start(par_rows[0:4, cols], q_right).then_inc(par_loaded, 16)
                sp.dma_start(par_rows[4:6, cols], cond).then_inc(par_loaded, 16)
                sp.dma_start(par_rows[6:7, cols], gate[0, 0]).then_inc(par_loaded, 16)
            for w, bias in enumerate((g1b, b1b, g2b, b2b)):
                sp.dma_start(par_rows[7 + 2 * w:9 + 2 * w, :],
                             bias.rearrange("(k p) -> k p", p=P)).then_inc(par_loaded, 16)

            def load_x(c):
                sp.dma_start(x_in[c % 2][:, :, :],
                             x[c // BCH, (c % BCH) * CW:(c % BCH + 1) * CW, :].rearrange("(t p) d -> p t d", p=P)
                             ).then_inc(x_loaded[c], 16)

            load_x(0)
            for i, w in enumerate((wq, wk, wv, wo)):
                sp.dma_start(w_raw[:, i, :, :], w.rearrange("(t p) d -> p t d", p=P)).then_inc(w_loaded, 16)
            load_x(1)
            sp.dma_start(cond_bc[:, :, :], cond.partition_broadcast(P)).then_inc(cond_loaded, 16)
            for w, weight in enumerate((g1w, b1w, g2w, b2w)):
                sp.dma_start(gw[:, 2 * w:2 * w + 2, :],
                             weight.rearrange("(k p) d -> p k d", p=P)).then_inc(cond_loaded, 16)

            def save_parts(c):
                for j in range(4):
                    sp.wait_ge(parts_ready, 4 * c + j + 1)
                    ch = (j % 2) * P
                    sp.dma_start(scr_qk[j // 2, :, ch:ch + P, c * CW:(c + 1) * CW].rearrange("a p t -> p a t"),
                                 qk_parts[j][:, :, :]).then_inc(parts_saved[j], 16)

            def load_stack(g):
                b, hg = g // (NG // BATCH), g % (NG // BATCH)
                if g >= SLOTS:
                    sp.wait_ge(pv_done, (g - SLOTS + 1) * NHALF * LT)
                for j in range(4):
                    sp.wait_ge(parts_saved[j], 16 * BCH * (b + 1))
                ch, tok = slice(hg * GH * DH, (hg + 1) * GH * DH), slice(b * SEQ, (b + 1) * SEQ)
                row = 0
                for part, times in Q_PARTS:
                    for _ in range(times):
                        sp.dma_start(q_st[g % SLOTS][row:row + DH, :, :],
                                     scr_qk[0, part, ch, tok].rearrange("(h d) t -> d h t", d=DH)
                                     ).then_inc(stack_loaded[g % SLOTS], 16)
                        row += DH
                for i, part in enumerate(K_PARTS):
                    sp.dma_start(k_st[g % SLOTS][i * DH:(i + 1) * DH, :, :],
                                 scr_qk[1, part, ch, tok].rearrange("(h d) t -> d h t", d=DH)
                                 ).then_inc(stack_loaded[g % SLOTS], 16)

            def load_max(g):
                sp.wait_ge(max_used, max_no["T", g] + 1)
                sp.dma_start(scr_max[g].rearrange("a (q l) -> (a q) l", l=P), nmax_t[:, :]).then_inc(nmax_saved, 16)
                sp.wait_ge(nmax_saved, 16 * (g + 1))
                sp.dma_start(q_st[g % SLOTS][PROD_ROWS:ALL_ROWS, :, :].rearrange("a h l -> a (h l)"),
                             scr_max[g]).then_inc(max_loaded[g % SLOTS], 16)

            for c in range(2, NCH):
                wait_filled(sp, "x_T", c - 2, 1)
                load_x(c)
            for c in range(BCH):
                save_parts(c)
            load_stack(0)
            load_stack(1)
            for c in range(BCH, NCH):
                save_parts(c)
            load_stack(2)
            wait_filled(sp, "v", NCH - 1, 1)
            sp.wait_ge(parts_ready, 4 * NCH)
            for j in range(4):
                sp.wait_ge(parts_saved[j], 16 * NCH)
            for i, w in enumerate((gate_w, hid_w)):
                sp.dma_start(f_raw[:, i, :, :], w.rearrange("(t p) d -> p t d", p=P)).then_inc(f_loaded, 16)
            sp.dma_start(f_raw[:, 2, :, :].rearrange("p a d -> p (a d)").rearrange("p (t n) -> p t n", t=KT),
                         out_w.rearrange("(t p) n -> p t n", p=P)).then_inc(f_loaded, 16)
            load_max(0)
            for g in range(1, NG):
                if g + 1 >= SLOTS and g + 1 < NG:
                    if g + 1 > 2:
                        load_stack(g + 1)
                load_max(g)
            for c in range(NCH):
                for tt in range(CT):
                    wait_evacuated(sp, "out", c, tt)
                sp.dma_start(out[c // BCH, (c % BCH) * CW:(c % BCH + 1) * CW, :].rearrange("(t p) d -> p t d", p=P),
                             attn[:, c * CT:(c + 1) * CT, :]).then_inc(stored, 16)
            sp.wait_ge(stored, 16 * NCH)

        @block.gpsimd
        def _(pool):
            nc.gpsimd.memset(ident[:, :], 0.0).then_inc(pool_step, 1)
            pool.wait_ge(pool_step, 1)
            nc.gpsimd.affine_select(out=ident[:, :], in_=ident[:, :], compare_op=ALU.not_equal, fill=1.0, base=0,
                                    pattern=[[-1, P]], channel_multiplier=1).then_inc(consts_ready, 1)
            pool.wait_ge(consts_ready, 1)
            nc.gpsimd.tensor_tensor(diag64[:, :], ident[:, 0:QUAT], ident[:, QUAT:P], ALU.add).then_inc(consts_ready, 1)
            nc.gpsimd.tensor_copy(ident_bf[:, :], ident[:, :]).then_inc(consts_ready, 1)
            nc.gpsimd.memset(v_sb[:, :, :, DH:VW], 1.0).then_inc(consts_ready, 1)
            for i in range(SLOTS):
                pool.wait_ge(consts_ready, 4 + i)
                nc.gpsimd.memset(k_st[i][PROD_ROWS:ALL_ROWS, :, :], 1.0).then_inc(consts_ready, 1)

            pool.wait_ge(consts_ready, 4 + SLOTS)

            def low_part(c):
                for kt in range(KT):
                    pool.wait_ge(xn_hi_ready, KT * c + kt + 1)
                    nc.gpsimd.tensor_tensor(xn_lo[c % 2][:, kt, :], xf[:, kt, :],
                                            xn_hi[c % 2][:, kt, :].bitcast(f32), ALU.subtract
                                            ).then_inc(xn_lo_ready, 1)

            def qk_low_parts(c):
                for j in range(4):
                    n = 4 * c + j
                    rest = qk_rest[n % 2]
                    wait_evacuated(pool, "qk", c, j)
                    nc.gpsimd.tensor_copy(qk_parts[j][:, 1, :], rest[:, :]).then_inc(pool_step, 1)
                    pool.wait_ge(pool_step, 2 + n)
                    nc.gpsimd.tensor_tensor(qk_parts[j][:, 2, :], rest[:, :], qk_parts[j][:, 1, :],
                                            ALU.subtract).then_inc(parts_ready, 1)

            for what, c in prep_steps:
                if what == "xs_T":
                    low_part(c)
                elif what == "QKV":
                    qk_low_parts(c)
            for what, c in fin_steps:
                if what == "WO":
                    pool.wait_ge(squares_done, NT + CT * (c + 1))
                    t = slice(c * CT, (c + 1) * CT)
                    nc.gpsimd.tensor_tensor(x1[:, t, :], x1[:, t, :], attn[:, t, :], ALU.add).then_inc(x12_ready, 1)
                elif what == "y_T":
                    for kt in range(KT):
                        pool.wait_ge(yn_hi_ready, KT * c + kt + 1)
                        nc.gpsimd.tensor_tensor(yn_lo[c][:, kt, :], yn_f[:, kt, :],
                                                yn_hi[c][:, kt, :].bitcast(f32), ALU.subtract
                                                ).then_inc(yn_lo_ready, 1)
            for n in range(len(ffn_units)):
                pool.wait_ge(h_hi_ready, n + 1)
                nc.gpsimd.tensor_tensor(h_lo[n % 3][:, :], h_f[n % 2][:, :], h_hi[n % 3][:, :].bitcast(f32),
                                        ALU.subtract).then_inc(h_lo_ready, 1)

        @block.scalar
        def _(act):
            act.wait_ge(norms_summed, 1)
            nc.scalar.activation(small[:, 8:10], small[:, 6:8], ACT.Sqrt).then_inc(norms_rooted, 1)

            def copy_x_t(c):
                for kt in range(KT):
                    wait_filled(act, "x_T", c, kt)
                    if c >= 2 and kt == 0:
                        wait_filled(act, "L0", c - 2, 1)
                    nc.scalar.activation(x_t[c % 2][:, kt, :], bank_of("x_T", c, kt), ACT.Copy
                                         ).then_inc(free_sem("x_T", c, kt), 1)

            def sum_squares(norm, t, src):
                n = norm * NT + t
                if n >= 2:
                    act.wait_ge(squares_done, n - 1)
                nc.scalar.activation(squares[:, n % 2, :], src, ACT.Square, accum_out=sumsq[:, norm, t:t + 1]
                                     ).then_inc(squares_done, 1)

            def copy_x1(c):
                for pair in range(2):
                    t = c * CT + 2 * pair
                    src = bank_of("L0", c, pair).rearrange("p (t d) -> p t d", t=2)
                    wait_filled(act, "L0", c, pair)
                    for i in range(2):
                        sum_squares(0, t + i, src[:, i, :])
                    nc.scalar.activation(x1[:, t:t + 2, :], src, ACT.Copy).then_inc(free_sem("L0", c, pair), 1)

            def root(norm, c):
                act.wait_ge(ms_ready, NCH * norm + c + 1)
                t = slice(c * CT, (c + 1) * CT)
                nc.scalar.activation(rms[:, norm, t], sumsq[:, norm, t], ACT.Sqrt).then_inc(rms_ready, 1)

            def norm_affine(c):
                root(0, c)
                b = c // BCH
                act.wait_ge(gb_ready, 1)
                if c:
                    act.wait_ge(xn_lo_ready, KT * c)
                for kt in range(KT):
                    wait_filled(act, "xs_T", c, kt)
                    nc.scalar.activation(xf[:, kt, :], bank_of("xs_T", c, kt), ACT.Identity,
                                         scale=gb_col(b, 0, 0, kt), bias=gb_col(b, 0, 1, kt)
                                         ).then_inc(free_sem("xs_T", c, kt), 1)

            def qkv_out(c):
                for j in range(4):
                    wait_filled(act, "qk", c, j)
                    if c:
                        act.wait_ge(parts_saved[j], 16 * c)
                    nc.scalar.activation(qk_parts[j][:, 0, :], bank_of("qk", c, j), ACT.Copy,
                                         scale=DH ** -0.5 if j < 2 else 1.0).then_inc(part1_ready, 1)
                if c == 0:
                    act.wait_ge(consts_ready, 4)
                for pair in range(2):
                    t = c * CT + 2 * pair
                    wait_filled(act, "v", c, pair)
                    nc.scalar.activation(v_sb[:, t:t + 2, :, 0:DH],
                                         bank_of("v", c, pair).rearrange("p (t h d) -> p t h d", t=2, d=DH),
                                         ACT.Copy).then_inc(free_sem("v", c, pair), 1)

            for what, c in prep_steps:
                if what == "x_T":
                    copy_x_t(c)
                elif what == "W":
                    for i in range(4):
                        wait_filled(act, "w", i)
                        dst = w_hi[:, i, :, :] if i < 3 else wo_hi[:, :, :]
                        nc.scalar.activation(dst, bank_of("w", i).rearrange("p (k d) -> p k d", k=KT), ACT.Copy
                                             ).then_inc(w_hi_ready, 1)
                elif what == "L0":
                    copy_x1(c)
                elif what == "xs_T":
                    norm_affine(c)
                else:
                    qkv_out(c)

            wait_filled(act, "v", NCH - 1, 1)
            act.wait_ge(parts_ready, 4 * NCH)
            for j in range(4):
                act.wait_ge(parts_saved[j], 16 * NCH)
            for s in range(NSTEP + 1):
                if s < NSTEP:
                    for h in range(GH):
                        e = GH * s + h
                        act.wait_ge(scores_filled, e + 1)
                        if s >= PR // GH and h == 0:
                            act.wait_ge(pv_done, s - PR // GH + 1)
                        nc.scalar.activation(prob[e % PR][:, :], e_bank(e), ACT.Exp).then_inc(exp_done, 1)
                if s and s % LT == 0:
                    o = s // LT - 1
                    act.wait_ge(pv_done, s)
                    if o >= 2:
                        act.wait_ge(max_filled, max_no["O", o - 2] + 1)
                    nc.scalar.activation(ot[o % 2][:, :], O_BANK, ACT.Copy).then_inc(o_copied, 1)

            for what, c in fin_steps:
                if what == "a_T":
                    for kt in range(KT):
                        wait_filled(act, "a_T", c, kt)
                        if c and kt == 0:
                            wait_filled(act, "WO", c - 1, 1)
                        nc.scalar.activation(at_hi[:, kt, :], bank_of("a_T", c, kt), ACT.Copy
                                             ).then_inc(at_hi_ready, 1)
                elif what == "WO":
                    for pair in range(2):
                        wait_evacuated(act, "WO", c, pair)
                        for i in range(2):
                            t = c * CT + 2 * pair + i
                            sum_squares(1, t, attn[:, t, :])
                elif what == "FW":
                    for n in range(3 * c, 3 * c + 3):
                        wait_filled(act, "fw", n)
                        nc.scalar.activation(fw_dst(n, 0), fw_src(n), ACT.Copy).then_inc(fw_hi_ready, 1)
                else:
                    root(1, c)
                    b = c // BCH
                    if c:
                        act.wait_ge(yn_lo_ready, KT * c)
                    for kt in range(KT):
                        wait_filled(act, "y_T", c, kt)
                        nc.scalar.activation(yn_f[:, kt, :], bank_of("y_T", c, kt), ACT.Identity,
                                             scale=gb_col(b, 1, 0, kt), bias=gb_col(b, 1, 1, kt)
                                             ).then_inc(free_sem("y_T", c, kt), 1)

            def high_hidden(n):
                wait_evacuated(act, "hid", n)
                if n >= 3:
                    wait_h_used(act, n - 3)
                nc.scalar.activation(h_hi[n % 3][:, :], h_f[n % 2][:, :], ACT.Copy).then_inc(h_hi_ready, 1)

            for n in range(len(ffn_units)):
                wait_filled(act, "gate", n)
                if n >= 2:
                    wait_evacuated(act, "hid", n - 2)
                nc.scalar.activation(silu_g[n % 2][:, :], bank_of("gate", n), ACT.Silu
                                     ).then_inc(free_sem("gate", n), 1)
                if n:
                    high_hidden(n - 1)
            high_hidden(len(ffn_units) - 1)

        @block.vector
        def _(dve):
            steps = [0]

            def link(ins):
                steps[0] += 1
                ins.then_inc(vector_step, 1)
                dve.wait_ge(vector_step, steps[0])

            wait_filled(dve, "par")
            nc.vector.tensor_copy(qc[:, :], bank_of("par")[:, 0:15]).then_inc(free_sem("par"), 1)
            wait_evacuated(dve, "par")
            link(nc.vector.tensor_tensor(small[:, 0:6], qc[:, 0:6], qc[:, 0:6], ALU.mult))
            nc.vector.reduce_sum(small[:, 6:7], small[:, 0:4], AX.X)
            link(nc.vector.reduce_sum(small[:, 7:8], small[:, 4:6], AX.X))
            nc.vector.tensor_scalar_add(small[:, 6:8], small[:, 6:8], QEPS).then_inc(norms_summed, 1)
            dve.wait_ge(norms_rooted, 1)
            link(nc.vector.reciprocal(small[:, 10:12], small[:, 8:10]))
            link(nc.vector.tensor_scalar(small[:, 12:16], qc[:, 0:4], small[:, 10:11], qc[:, 6:7], ALU.mult, ALU.mult))
            nc.vector.tensor_scalar(small[:, 16:20], small[:, 12:16], -1.0, None, ALU.mult)
            link(nc.vector.tensor_scalar(small[:, 20:22], qc[:, 4:6], small[:, 11:12], None, ALU.mult))
            right = small[:, 24:32].rearrange("p (t k) -> p t k", t=KT)
            signed = ((0, 5, 6, 7), (1, 0, 3, 6), (2, 7, 0, 1), (3, 2, 5, 0))
            for j, row in enumerate(signed):
                part = slice(QUAT * (j % 2), QUAT * (j % 2) + QUAT)
                for k, i in enumerate(row):
                    last = nc.vector.tensor_copy(right[part, j // 2, k:k + 1], small[part, 12 + i:13 + i])
            link(last)
            tmp = small[:, 32:40].rearrange("p (t k) -> p t k", t=KT)
            cross = small[:, 40:48].rearrange("p (t k) -> p t k", t=KT)

            def r(k):
                return right[:, :, k:k + 1]

            for k, (a, b, op) in enumerate(((1, 2, ALU.add), (3, 2, ALU.subtract), (1, 3, ALU.subtract),
                                            (2, 1, ALU.subtract))):
                last = nc.vector.tensor_tensor(tmp[:, :, k:k + 1], r(a), r(b), op)
            link(last)
            nc.vector.scalar_tensor_tensor(out=cross[:, :, 0:1], in0=tmp[:, :, 0:1], scalar=-1.0, in1=r(3),
                                           op0=ALU.mult, op1=ALU.subtract)
            link(nc.vector.tensor_tensor(cross[:, :, 1:4], tmp[:, :, 1:4], r(0).to_broadcast([P, KT, 3]), ALU.add))
            link(nc.vector.tensor_scalar(small[:, 48:56], small[:, 40:48], small[:, 21:22], None, ALU.mult))
            link(nc.vector.scalar_tensor_tensor(out=small[:, 56:64], in0=small[:, 24:32], scalar=small[:, 20:21],
                                                in1=small[:, 48:56], op0=ALU.mult, op1=ALU.add))
            dve.wait_ge(consts_ready, 2)
            rot_blocks = rot[:, :, :].rearrange("p t (k c) -> p (t k) c", c=QUAT)
            link(nc.vector.tensor_tensor(rot_blocks, diag64[:, :].unsqueeze(1).to_broadcast([P, 8, QUAT]),
                                         small[:, 56:64].unsqueeze(2).to_broadcast([P, 8, QUAT]), ALU.mult))
            for kt in range(KT):
                diag = rot[:, kt, kt * P:(kt + 1) * P]
                last = nc.vector.tensor_tensor(diag, diag, ident[:, :], ALU.add)
            last.then_inc(rot_ready, 1)

            for i in range(4):
                wait_filled(dve, "w", i)
                dve.wait_ge(w_hi_ready, i + 1)
                hi, lo = (w_hi[:, i, :, :], w_lo[:, i, :, :]) if i < 3 else (wo_hi[:, :, :], wo_lo[:, :, :])
                nc.vector.tensor_tensor(lo, bank_of("w", i).rearrange("p (k d) -> p k d", k=KT), hi.bitcast(f32),
                                        ALU.subtract).then_inc(free_sem("w", i), 1)

            dve.wait_ge(cond_loaded, 16 * 5)
            for b in range(BATCH):
                link(nc.vector.tensor_tensor(gprod[:, :, :], gw[:, :, :],
                                             cond_bc[:, b:b + 1, :].to_broadcast([P, 8, DT]), ALU.mult))
                link(nc.vector.reduce_sum(gb[:, b, :], gprod[:, :, :], AX.X))
                last = nc.vector.tensor_tensor(gb[:, b, :], gb[:, b, :], qc[:, 7:15], ALU.add)
            last.then_inc(gb_ready, 1)
            dve.wait_ge(gb_ready, 1)

            def scale_tokens(norm, c, src, dst, ready):
                t = slice(c * CT, (c + 1) * CT)
                nc.vector.tensor_scalar(sumsq[:, norm, t], sumsq[:, norm, t], 1.0 / D, NEPS, ALU.mult, ALU.add
                                        ).then_inc(ms_ready, 1)
                dve.wait_ge(rms_ready, NCH * norm + c + 1)
                link(nc.vector.reciprocal(inv_rms[:, norm, t], rms[:, norm, t]))
                for i in range(CT):
                    n = c * CT + i
                    last = nc.vector.tensor_scalar(dst[:, i, :], src[:, n, :], inv_rms[:, norm, n:n + 1], None,
                                                   ALU.mult)
                last.then_inc(ready, 1)

            for what, c in prep_steps:
                if what == "xs_T":
                    for pair in range(2):
                        wait_evacuated(dve, "L0", c, pair)
                    if c >= 2:
                        wait_filled(dve, "xs_T", c - 2, 1)
                    scale_tokens(0, c, x1, xs[c % 2], xs_ready)
                    if c >= 2:
                        wait_filled(dve, "v", c - 2, 1)
                    for kt in range(KT):
                        wait_evacuated(dve, "xs_T", c, kt)
                        nc.vector.tensor_copy(xn_hi[c % 2][:, kt, :], xf[:, kt, :]).then_inc(xn_hi_ready, 1)
                elif what == "QKV":
                    for j in range(4):
                        n = 4 * c + j
                        dve.wait_ge(part1_ready, n + 1)
                        if n >= 2:
                            dve.wait_ge(parts_ready, n - 1)
                        nc.vector.scalar_tensor_tensor(out=qk_rest[n % 2][:, :], in0=bank_of("qk", c, j),
                                                       scalar=DH ** -0.5 if j < 2 else 1.0,
                                                       in1=qk_parts[j][:, 0, :], op0=ALU.mult, op1=ALU.subtract
                                                       ).then_inc(free_sem("qk", c, j), 1)

            if prep_total[7]:
                dve.wait_ge(evacuated[7], prep_total[7])
            nc.vector.memset(O_BANK, 0.0).then_inc(o_cleared, 1)
            wait_filled(dve, "v", NCH - 1, 1)
            dve.wait_ge(parts_ready, 4 * NCH)
            for j in range(4):
                dve.wait_ge(parts_saved[j], 16 * NCH)
            for s in range(-1, NSTEP + 2):
                for item in max_items(s):
                    what, n = item
                    slot = max_slot(item)
                    dve.wait_ge(max_filled, max_no[item] + 1)
                    if what == "max":
                        g, h, lt = n // GU, n % GU // LT, n % LT
                        nc.vector.tensor_reduce(out=nmax[:, g % 2, h, lt:lt + 1], in_=slot, axis=AX.XY, op=ALU.max,
                                                negate=True).then_inc(max_used, 1)
                        if n % GU == GU - 1:
                            all_max = nmax[:, g % 2, :, :].rearrange("p h t -> p (h t)")
                            dve.wait_ge(max_used, max_no[item] + 1)
                            link(nc.vector.tensor_copy(nmax_parts[:, 0, :], all_max))
                            link(nc.vector.tensor_tensor(nmax_rest[:, :], all_max, nmax_parts[:, 0, :], ALU.subtract))
                            link(nc.vector.tensor_copy(nmax_parts[:, 1, :], nmax_rest[:, :]))
                            nc.vector.tensor_tensor(nmax_parts[:, 2, :], nmax_rest[:, :], nmax_parts[:, 1, :],
                                                    ALU.subtract).then_inc(nmax_split, 1)
                    elif what == "T":
                        if n:
                            dve.wait_ge(nmax_saved, 16 * n)
                        nc.vector.tensor_copy(nmax_t[:, :], slot[0:3 * GU, 0, 0:P // 2].bitcast(bf16)
                                              ).then_inc(max_used, 1)
                    else:
                        o = slot[:, 0, :].rearrange("p (t h d) -> p t h d", t=CT, h=GH)
                        g, half = n // NHALF, n % NHALF
                        b, hg = g // (NG // BATCH), g % (NG // BATCH)
                        t = b * LT + half * CT
                        if n:
                            dve.wait_ge(max_used, max_no["O", n - 1] + 1)
                        link(nc.vector.reciprocal(rsum[:, :, :, :], o[:, :, :, DH:VW]))
                        nc.vector.tensor_tensor(
                            attn[:, t:t + CT, hg * GH * DH:(hg + 1) * GH * DH].rearrange("p t (h d) -> p t h d", d=DH),
                            o[:, :, :, 0:DH], rsum[:, :, :, :].to_broadcast([P, CT, GH, DH]), ALU.mult
                        ).then_inc(max_used, 1)

            for what, c in fin_steps:
                if what == "a_T":
                    for kt in range(KT):
                        dve.wait_ge(at_hi_ready, KT * c + kt + 1)
                        nc.vector.tensor_tensor(at_lo[:, kt, :], bank_of("a_T", c, kt), at_hi[:, kt, :].bitcast(f32),
                                                ALU.subtract).then_inc(free_sem("a_T", c, kt), 1)
                elif what == "WO":
                    for pair in range(2):
                        t = c * CT + 2 * pair
                        wait_filled(dve, "WO", c, pair)
                        nc.vector.tensor_tensor(attn[:, t:t + 2, :],
                                                bank_of("WO", c, pair).rearrange("p (t d) -> p t d", t=2),
                                                x1[:, t:t + 2, :], ALU.add).then_inc(free_sem("WO", c, pair), 1)
                elif what == "FW":
                    for n in range(3 * c, 3 * c + 3):
                        dve.wait_ge(fw_hi_ready, n + 1)
                        nc.vector.tensor_tensor(fw_dst(n, 1), fw_src(n), fw_dst(n, 0).bitcast(f32), ALU.subtract
                                                ).then_inc(free_sem("fw", n), 1)
                else:
                    dve.wait_ge(squares_done, NT + CT * (c + 1))
                    if c:
                        wait_filled(dve, "y_T", c - 1, 1)
                    scale_tokens(1, c, attn, xs2, ys_ready)
                    for kt in range(KT):
                        wait_evacuated(dve, "y_T", c, kt)
                        nc.vector.tensor_copy(yn_hi[c][:, kt, :], yn_f[:, kt, :]).then_inc(yn_hi_ready, 1)
            for n in range(len(ffn_units) + OUT_LAG):
                if n < len(ffn_units):
                    wait_evacuated(dve, "gate", n)
                    wait_filled(dve, "hid", n)
                    if n >= 2:
                        dve.wait_ge(h_lo_ready, n - 1)
                    nc.vector.tensor_tensor(h_f[n % 2][:, :], bank_of("hid", n), silu_g[n % 2][:, :], ALU.mult
                                            ).then_inc(free_sem("hid", n), 1)
                if n >= OUT_LAG and ffn_units[n - OUT_LAG][1] == HT - 1:
                    c = ffn_units[n - OUT_LAG][0]
                    dve.wait_ge(x12_ready, c + 1)
                    for tt in range(CT):
                        wait_filled(dve, "out", c, tt)
                        nc.vector.tensor_tensor(attn[:, c * CT + tt, :], bank_of("out", c, tt)[:, 0:D],
                                                x1[:, c * CT + tt, :], ALU.add).then_inc(free_sem("out", c, tt), 1)

        @block.tensor
        def _(pe):
            def transposes(key, srcs):
                wait_bank(pe, *key)
                for i, src in enumerate(srcs):
                    last = nc.tensor.transpose(bank_of(*key)[:, i * P:(i + 1) * P], src, ident[:, :])
                last.then_inc(tile_filled, 1)

            def split_product(dst, stationary, moving, first=True, last=True):
                passes = [(s, m) for (sh, sl), (mh, ml) in zip(stationary, moving)
                          for s, m in ((sl, mh), (sh, ml), (sh, mh))]
                for i, (s, m) in enumerate(passes):
                    ins = nc.tensor.matmul(dst, s, m, start=first and i == 0, stop=last and i == len(passes) - 1)
                return ins

            pe.wait_ge(consts_ready, 1)
            pe.wait_ge(par_loaded, 16 * 10)
            nc.tensor.transpose(bank_of("par")[:, 0:15], par_rows[:, :], ident[0:15, 0:15]).then_inc(tile_filled, 1)

            for what, c in prep_steps:
                if what == "x_T":
                    pe.wait_ge(x_loaded[c], 16)
                    for kt in range(KT):
                        transposes(("x_T", c, kt), [x_in[c % 2][:, t, kt * P:(kt + 1) * P] for t in range(CT)])
                elif what == "W":
                    pe.wait_ge(w_loaded, 16 * 4)
                    for i in range(4):
                        transposes(("w", i), [w_raw[:, i, ot_, kt * P:(kt + 1) * P]
                                              for kt in range(KT) for ot_ in range(KT)])
                elif what == "L0":
                    if c == 0:
                        pe.wait_ge(rot_ready, 1)
                    for kt in range(KT):
                        wait_evacuated(pe, "x_T", c, kt)
                    for pair in range(2):
                        wait_bank(pe, "L0", c, pair)
                        for i in range(2):
                            t = 2 * pair + i
                            for kt in range(KT):
                                last = nc.tensor.matmul(bank_of("L0", c, pair)[:, i * D:(i + 1) * D],
                                                        x_t[c % 2][:, kt, t * P:(t + 1) * P], rot[:, kt, :],
                                                        start=kt == 0, stop=kt == KT - 1)
                        last.then_inc(tile_filled, 1)
                elif what == "xs_T":
                    pe.wait_ge(xs_ready, c + 1)
                    for kt in range(KT):
                        transposes(("xs_T", c, kt), [xs[c % 2][:, t, kt * P:(kt + 1) * P] for t in range(CT)])
                else:
                    hi, lo = xn_hi[c % 2], xn_lo[c % 2]
                    if c == 0:
                        for i in range(3):
                            wait_evacuated(pe, "w", i)
                    for kt in range(KT):
                        wait_evacuated(pe, "xs_T", c, kt)
                    pe.wait_ge(xn_lo_ready, KT * (c + 1))
                    for j in range(4):
                        wait_bank(pe, "qk", c, j)
                        cols = slice((j % 2) * P, (j % 2 + 1) * P)
                        split_product(bank_of("qk", c, j),
                                      [(w_hi[:, j // 2, kt, cols], w_lo[:, j // 2, kt, cols]) for kt in range(KT)],
                                      [(hi[:, kt, :], lo[:, kt, :]) for kt in range(KT)]).then_inc(tile_filled, 1)
                    for pair in range(2):
                        wait_bank(pe, "v", c, pair)
                        for i in range(2):
                            t = slice((2 * pair + i) * P, (2 * pair + i + 1) * P)
                            last = split_product(bank_of("v", c, pair)[:, i * D:(i + 1) * D],
                                                 [(hi[:, kt, t], lo[:, kt, t]) for kt in range(KT)],
                                                 [(w_hi[:, 2, kt, :], w_lo[:, 2, kt, :]) for kt in range(KT)])
                        last.then_inc(tile_filled, 1)

            for i in range(8):
                if prep_total[i]:
                    pe.wait_ge(evacuated[i], prep_total[i])
            pe.wait_ge(consts_ready, 4 + SLOTS)

            def operands_loaded(g):
                pe.wait_ge(stack_loaded[g % SLOTS], 16 * 2 * len(K_PARTS) * (g // SLOTS + 1))

            def do_item(item):
                what, n = item
                slot = max_slot(item)
                if max_no[item] >= 2:
                    pe.wait_ge(max_used, max_no[item] - 1)
                if what == "max":
                    g, h, lt = n // GU, n % GU // LT, n % LT
                    if n % GU == 0:
                        operands_loaded(g)
                    for half in range(SEQ // 512):
                        last = nc.tensor.matmul(slot[:, half, :], q_st[g % SLOTS][0:PROD_ROWS, h, lt * P:(lt + 1) * P],
                                                k_st[g % SLOTS][0:PROD_ROWS, h, half * 512:(half + 1) * 512],
                                                start=True, stop=True)
                elif what == "T":
                    pe.wait_ge(nmax_split, n + 1)
                    last = nc.tensor.transpose(slot[0:3 * GU, 0, 0:P // 2].bitcast(bf16),
                                               nmax_parts[:, :, :].rearrange("p a q -> p (a q)"), ident_bf[:, :])
                else:
                    pe.wait_ge(o_copied, n + 1)
                    for t in range(CT):
                        last = nc.tensor.transpose(slot[:, 0, t * P:(t + 1) * P], ot[n % 2][:, t * P:(t + 1) * P],
                                                   ident[:, :])
                last.then_inc(max_filled, 1)

            def scores(s, h):
                g, half, kt = s // (NHALF * LT), s // LT % NHALF, s % LT
                e = GH * s + h
                if e >= EB:
                    pe.wait_ge(exp_done, e - EB + 1)
                if s % (NHALF * LT) == 0 and h == 0:
                    pe.wait_ge(max_loaded[g % SLOTS], 16 * (g // SLOTS + 1))
                nc.tensor.matmul(e_bank(e), k_st[g % SLOTS][0:ALL_ROWS, h, kt * P:(kt + 1) * P],
                                 q_st[g % SLOTS][0:ALL_ROWS, h, half * HALF:(half + 1) * HALF],
                                 start=True, stop=True).then_inc(scores_filled, 1)

            def values(s):
                g, kt = s // (NHALF * LT), s % LT
                b, hg = g // (NG // BATCH), g % (NG // BATCH)
                pe.wait_ge(exp_done, GH * (s + 1))
                if kt == 0:
                    if s:
                        pe.wait_ge(o_copied, s // LT)
                    else:
                        pe.wait_ge(o_cleared, 1)
                for h in range(GH):
                    last = nc.tensor.matmul(O_BANK[32 * h:32 * h + VW, :], v_sb[:, b * LT + kt, hg * GH + h, :],
                                            prob[(GH * s + h) % PR][:, :], start=kt == 0, stop=kt == LT - 1)
                last.then_inc(pv_done, 1)

            for item in max_items(-1):
                do_item(item)
            for s in range(NSTEP + 2):
                if s < NSTEP:
                    for h in range(GH - 1):
                        scores(s, h)
                items = max_items(s)
                for item in items[:-1]:
                    do_item(item)
                if 1 <= s <= NSTEP:
                    values(s - 1)
                if s < NSTEP:
                    scores(s, GH - 1)
                for item in items[-1:]:
                    do_item(item)

            pe.wait_ge(max_used, len(max_no))
            pe.wait_ge(exp_done, GH * NSTEP)
            pe.wait_ge(o_copied, NG * NHALF)
            pe.wait_ge(f_loaded, 16 * 3)
            for what, c in fin_steps:
                if what == "a_T":
                    for kt in range(KT):
                        transposes(("a_T", c, kt), [attn[:, c * CT + t, kt * P:(kt + 1) * P] for t in range(CT)])
                elif what == "WO":
                    for kt in range(KT):
                        wait_evacuated(pe, "a_T", c, kt)
                    for pair in range(2):
                        wait_bank(pe, "WO", c, pair)
                        for i in range(2):
                            t = slice((2 * pair + i) * P, (2 * pair + i + 1) * P)
                            last = split_product(bank_of("WO", c, pair)[:, i * D:(i + 1) * D],
                                                 [(at_hi[:, kt, t], at_lo[:, kt, t]) for kt in range(KT)],
                                                 [(wo_hi[:, kt, :], wo_lo[:, kt, :]) for kt in range(KT)])
                        last.then_inc(tile_filled, 1)
                elif what == "FW":
                    for n in range(3 * c, 3 * c + 3):
                        if n < 8:
                            w, kt, half = n // 4, n // 2 % 2, n % 2
                            srcs = [f_raw[:, w, 4 * half + r, kt * P:(kt + 1) * P] for r in range(4)]
                        else:
                            raw = f_raw[:, 2, :, :].rearrange("p a d -> p (a d)").rearrange("p (t n) -> p t n", t=KT)
                            ht = 2 * (n - 8)
                            srcs = [raw[:, ot_, (ht + a) * P:(ht + a + 1) * P] for a in range(2) for ot_ in range(KT)]
                        transposes(("fw", n), srcs)
                else:
                    pe.wait_ge(ys_ready, c + 1)
                    for kt in range(KT):
                        transposes(("y_T", c, kt), [xs2[:, t, kt * P:(kt + 1) * P] for t in range(CT)])
            for n in range(12):
                wait_evacuated(pe, "fw", n)
            for n in range(len(ffn_units) + OUT_LAG):
                if n < len(ffn_units):
                    c, ht = ffn_units[n]
                    if ht == 0:
                        for kt in range(KT):
                            wait_evacuated(pe, "y_T", c, kt)
                        pe.wait_ge(yn_lo_ready, KT * (c + 1))
                    cols = slice(ht * P, (ht + 1) * P)
                    for w, name in enumerate(("gate", "hid")):
                        wait_bank(pe, name, n)
                        split_product(bank_of(name, n),
                                      [(fw_hi[:, w, kt, cols], fw_lo[:, w, kt, cols]) for kt in range(KT)],
                                      [(yn_hi[c][:, kt, :], yn_lo[c][:, kt, :]) for kt in range(KT)]
                                      ).then_inc(tile_filled, 1)
                if n >= OUT_LAG:
                    m = n - OUT_LAG
                    c, ht = ffn_units[m]
                    pe.wait_ge(h_lo_ready, m + 1)
                    for tt in range(CT):
                        if ht == 0:
                            wait_bank(pe, "out", c, tt)
                        t = slice(tt * P, (tt + 1) * P)
                        ins = split_product(bank_of("out", c, tt)[:, 0:D], [(h_hi[m % 3][:, t], h_lo[m % 3][:, t])],
                                            [(fo_hi[:, ht, :], fo_lo[:, ht, :])], ht == 0, ht == HT - 1)
                        if ht == HT - 1:
                            ins.then_inc(tile_filled, 1)
                    if ht < HT - 1:
                        ins.then_inc(h_used, 1)


NAMES = ["x", "cond_256", "L0_cond_q_right", "L0_cond_spectral_gate", "L1_cond_Wq", "L1_cond_Wk", "L1_cond_Wv",
         "L1_cond_Wo", "L1_cond_g1w", "L1_cond_g1b", "L1_cond_b1w", "L1_cond_b1b", "L1_cond_g2w", "L1_cond_g2b",
         "L1_cond_b2w", "L1_cond_b2b", "L1_cond_gate_w", "L1_cond_hid_w", "L1_cond_out_w"]


def kernel(**inputs):
    import numpy as _np
    import concourse.bacc as _bacc
    from concourse import mybir as _mybir
    from concourse.bass_utils import run_bass_kernel_spmd as _run

    nc = _bacc.Bacc("TRN2", target_bir_lowering=False, num_devices=1)
    arrays, args = {}, []
    for name in NAMES:
        a = _np.ascontiguousarray(inputs[name])
        arrays[f"in_{name}"] = a
        args.append(nc.dram_tensor(f"in_{name}", a.shape, _mybir.dt.from_np(a.dtype), kind="ExternalInput").ap())
    args.append(nc.dram_tensor("out_x", (BATCH, SEQ, D), _mybir.dt.float32, kind="ExternalOutput").ap())
    build(nc, *args)
    r = _run(nc, [arrays], core_ids=[0])
    return r.results[0]["out_x"]
```

```python
import concourse.bass as bass
from concourse import mybir
from contextlib import ExitStack

P = 128
BATCH, SEQ, D = 2, 1024, 256
HEADS, DH = 16, 16
HIDDEN = 1024
QUAT = D // 4
DT = 64
TOK = BATCH * SEQ
NT = TOK // P
CT = 4
CW = CT * P
NCH = NT // CT
BCH = NCH // BATCH
KT = D // P
GH = 4
NG = BATCH * HEADS // GH
LT = SEQ // P
HALF = 512
NHALF = SEQ // HALF
HT_Q = HALF // P
VW = DH + 1
Q_PARTS = ((0, 3), (1, 2), (2, 1))
K_PARTS = (0, 1, 2, 0, 1, 0)
PROD_ROWS = DH * len(K_PARTS)
ALL_ROWS = PROD_ROWS + 3
SLOTS = 3
EB = 3
PR = 8
LEAD = 10
HT = HIDDEN // P
QEPS, NEPS = 1e-8, 1e-6


def build(nc, x, cond, q_right, gate, wq, wk, wv, wo, g1w, g1b, b1w, b1b, g2w, g2b, b2w, b2b,
          gate_w, hid_w, out_w, out):
    f32, f32r, bf16 = mybir.dt.float32, mybir.dt.float32r, mybir.dt.bfloat16
    ALU, ACT, AX = mybir.AluOpType, mybir.ActivationFunctionType, mybir.AxisListType

    ctx = ExitStack()
    with ctx:
        def sb(name, shape, dt, scope=None):
            return (scope or ctx).enter_context(nc.sbuf_tensor(name, shape, dt))

        def sem(name):
            return ctx.enter_context(nc.semaphore(name))

        ident = sb("ident", [P, P], f32)
        ident_bf = sb("ident_bf", [P, P], bf16)
        x1 = sb("x1", [P, NT, D], f32)
        attn = sb("attn", [P, NT, D], f32)
        wo_hi, wo_lo = (sb(f"wo_{s}", [P, KT, D], f32r) for s in ("hi", "lo"))
        gb = sb("gb", [P, BATCH, 8], f32)
        sumsq = sb("sumsq", [P, 2, NT], f32)
        ms = sb("ms", [P, 2, NT], f32)
        inv_rms = sb("inv_rms", [P, 2, NT], f32)
        neg_half = sb("neg_half", [P, CT], f32)
        qc = sb("qc", [P, 15], f32)
        squares = sb("squares", [P, 2, D], bf16)

        nmax = sb("nmax", [P, 2, GH, HT_Q], f32)
        nmax_rest = sb("nmax_rest", [P, GH * HT_Q], f32)
        nmax_parts = sb("nmax_parts", [P, 3, GH * HT_Q], bf16)
        nmax_t = sb("nmax_t", [3 * GH * HT_Q, P], bf16)
        rsum = sb("rsum", [P, CT, GH, 1], f32)

        scope_b = ExitStack()
        v_sb = sb("v_sb", [P, NT, HEADS, VW], f32, scope_b)
        q_st = [sb(f"q_st{i}", [P, GH, SEQ], bf16, scope_b) for i in range(SLOTS)]
        k_st = [sb(f"k_st{i}", [P, GH, SEQ], bf16, scope_b) for i in range(SLOTS)]

        scope_p = ExitStack()
        par_rows = sb("par_rows", [15, P], f32, scope_p)
        cond_bc = sb("cond_bc", [P, BATCH, DT], f32, scope_p)
        gw = sb("gw", [P, 8, DT], f32, scope_p)
        gprod = sb("gprod", [P, 8, DT], f32, scope_p)
        diag64 = sb("diag64", [P, QUAT], f32, scope_p)
        small = sb("small", [P, 64], f32, scope_p)
        rot = sb("rot", [P, KT, D], f32, scope_p)
        w_raw = sb("w_raw", [P, 4, KT, D], f32, scope_p)
        w_hi = sb("w_hi", [P, 3, KT, D], f32r, scope_p)
        w_lo = sb("w_lo", [P, 3, KT, D], f32r, scope_p)
        ones_row = sb("ones_row", [3, SEQ], bf16, scope_p)
        x_in = [sb(f"x_in{i}", [P, CT, D], f32, scope_p) for i in range(2)]
        x_t = [sb(f"x_t{i}", [P, KT, CW], f32, scope_p) for i in range(2)]
        xs = [sb(f"xs{i}", [P, CT, D], f32, scope_p) for i in range(2)]
        xf = sb("xf", [P, KT, CW], f32, scope_p)
        xn_hi = [sb(f"xn_hi{i}", [P, KT, CW], f32r, scope_p) for i in range(2)]
        xn_lo = [sb(f"xn_lo{i}", [P, KT, CW], f32r, scope_p) for i in range(2)]
        qk_rest = [sb(f"qk_rest{i}", [P, CW], f32, scope_p) for i in range(3)]
        qk_parts = [sb(f"qk_parts{i}", [P, 3, CW], bf16, scope_p) for i in range(4)]
        scope_p.close()

        prob = [sb(f"prob{i}", [P, HALF], f32, scope_b) for i in range(PR)]
        ot = sb("ot", [P, HALF], f32, scope_b)
        f_raw = sb("f_raw", [P, 4, D], f32, scope_b)
        fw_hi = sb("fw_hi", [P, 2, KT, HIDDEN], f32r, scope_b)
        fw_lo = sb("fw_lo", [P, 2, KT, HIDDEN], f32r, scope_b)
        fo_hi = sb("fo_hi", [P, HT, D], f32r, scope_b)
        fo_lo = sb("fo_lo", [P, HT, D], f32r, scope_b)
        at_hi = sb("at_hi", [P, KT, CW], f32r, scope_b)
        at_lo = sb("at_lo", [P, KT, CW], f32r, scope_b)
        xs2 = sb("xs2", [P, CT, D], f32, scope_b)
        yn_f = sb("yn_f", [P, KT, CW], f32, scope_b)
        yn_hi = [sb(f"yn_hi{i}", [P, KT, CW], f32r, scope_b) for i in range(BCH)]
        yn_lo = [sb(f"yn_lo{i}", [P, KT, CW], f32r, scope_b) for i in range(BCH)]
        scope_b.close()
        yn_hi += [sb(f"yn_hi{i}", [P, KT, CW], f32r) for i in range(BCH, NCH)]
        yn_lo += [sb(f"yn_lo{i}", [P, KT, CW], f32r) for i in range(BCH, NCH)]
        silu_g = [sb(f"silu_g{i}", [P, CW], f32) for i in range(2)]
        h_f = [sb(f"h_f{i}", [P, CW], f32) for i in range(2)]
        h_hi = [sb(f"h_hi{i}", [P, CW], f32r) for i in range(3)]
        h_lo = [sb(f"h_lo{i}", [P, CW], f32r) for i in range(3)]

        psum = ctx.enter_context(nc.psum_tensor("psum", [P, 8, 512], f32))
        scr_qk = nc.dram_tensor("scr_qk", (2, 3, D, TOK), bf16, kind="Internal").ap()
        scr_max = nc.dram_tensor("scr_max", (NG * NHALF, 3, GH * HALF), bf16, kind="Internal").ap()

        plan, bank_total = {}, [0] * 8
        before = {}

        def plan_tile(key, bank):
            before[key] = bank_total[bank]
            bank_total[bank] += 1
            plan[key] = (len(plan), bank, bank_total[bank])

        def qkv(c):
            return [("QK", c, j) for j in range(4)] + [("V", c, pair) for pair in range(2)]

        NSTEP = NG * NHALF * LT
        UNITS = NG * GH * LT
        GU = GH * LT
        HU = GH * HT_Q
        T_AT = 2
        first_items = ([("max", u) for u in range(HU + T_AT)] + [("T", 0)]
                       + [("max", u) for u in range(HU + T_AT, HU + LEAD)])

        def unit(u):
            half, h, t = u % GU // HU, u % HU // HT_Q, u % HT_Q
            return u // GU, h, half * HT_Q + t

        half_done = NSTEP // BATCH
        placed = {half_done + d: item for d, item in (
            (3, ("a_T", 0, 0)), (5, ("a_T", 0, 1)), (7, ("WO", 0, 0)), (9, ("WO", 0, 1)),
            (11, ("a_T", 1, 0)), (13, ("a_T", 1, 1)), (15, ("WO", 1, 0)), (18, ("WO", 1, 1)),
            (20, ("y_T", 0, 0)), (22, ("y_T", 0, 1)), (30, ("y_T", 1, 0)), (32, ("y_T", 1, 1)))}
        fw_first = half_done + 40
        for r in range(6):
            placed[fw_first + 4 * r] = ("FW", 2 * r)
            placed[fw_first + 4 * r + 1] = ("FW", 2 * r + 1)
        fw_loads = {fw_first - 6: 0} | {fw_first + 4 * r - 2: r for r in range(1, 6)}
        square_steps = {half_done + 9: (0, 0), half_done + 11: (0, 1), half_done + 17: (1, 0), half_done + 20: (1, 1)}
        mean_steps = {half_done + 13: 0, half_done + 22: 1}
        scale_steps = {half_done + 15: 0, half_done + 25: 1}

        def max_items(step):
            items = []
            if step % LT == 1 and step > LT:
                items.append(("O", step // LT - 1))
            if step in placed:
                items.append(placed[step])
            first = HU + LEAD + 2 * step
            if first % HU == T_AT and first // HU - 1 < NG * NHALF:
                items.append(("T", first // HU - 1))
            if first >= UNITS:
                return items
            return [("max", first)] + items + [("max", first + 1)]

        max_no = {}
        for item in first_items + [i for step in range(NSTEP + 2) for i in max_items(step)]:
            max_no[item] = len(max_no)

        prep = [("x_T", 0), ("W",), ("L0", 0), ("SC", 0), ("x_T", 1), ("L0", 1), ("SC", 1), ("xs_T", 0)]
        prep += [("x_T", 2), ("L0", 2), ("xs_T", 1)] + qkv(0)[:2] + [("SC", 2)] + qkv(0)[2:] + qkv(1)
        prep += [("switch",), ("xs_T", 2), ("x_T", 3), ("L0", 3), ("SC", 3)]
        tail, pending = qkv(2)[:2] + [("xs_T", 3)] + qkv(2)[2:] + qkv(3), list(first_items)
        for i, what in enumerate(tail):
            prep.append(what)
            take = -(-len(pending) // (len(tail) - i))
            prep += [("item", it) for it in pending[:take]]
            pending = pending[take:]

        ring, width = [0], [8]
        plan_tile(("par",), 7)

        def plan_ring(key):
            plan_tile(key, 8 - width[0] + ring[0] % width[0])
            ring[0] += 1

        before_items = [0] * 8
        for step in prep:
            if step[0] == "switch":
                before_items = list(bank_total)
                width[0], ring[0] = 4, 0
            elif step[0] == "W":
                for i in range(4):
                    plan_ring(("W", i))
            elif step[0] in ("x_T", "L0", "xs_T"):
                for i in range(2):
                    plan_ring((*step, i))
            elif step[0] in ("QK", "V"):
                plan_ring(step)
        prep_total = list(bank_total)

        OUT_LAG = 2
        ffn_units = [(c, ht) for c in range(NCH) for ht in range(HT)]
        fin = ([("F", 0), ("a_T", 2, 0), ("a_T", 2, 1), ("F", 1), ("WO", 2, 0), ("WO", 2, 1), ("F", 2),
                ("a_T", 3, 0), ("a_T", 3, 1), ("SC", 2), ("F", 3), ("WO", 3, 0), ("WO", 3, 1), ("F", 4),
                ("y_T", 2, 0), ("y_T", 2, 1), ("F", 5), ("SC", 3), ("F", 6), ("y_T", 3, 0), ("y_T", 3, 1)]
               + [("F", n) for n in range(7, len(ffn_units) + OUT_LAG)])
        for step in fin:
            if step[0] == "F":
                n = step[1]
                if n < len(ffn_units):
                    plan_ring(("gate", n))
                    plan_ring(("hid", n))
                if n >= OUT_LAG and ffn_units[n - OUT_LAG][1] == HT - 1:
                    for tt in range(CT):
                        plan_tile(("out", ffn_units[n - OUT_LAG][0], tt), tt)
            elif step[0] != "SC":
                plan_ring(step)

        par_loaded = sem("par_loaded")
        cond_loaded = sem("cond_loaded")
        w_loaded = sem("w_loaded")
        x_loaded = [sem(f"x_loaded{c}") for c in range(NCH)]
        f_loaded = sem("f_loaded")
        consts_ready = sem("consts_ready")
        tile_filled = sem("tile_filled")
        evacuated = [sem(f"evacuated{i}") for i in range(8)]
        vector_step = sem("vector_step")
        pool_step = sem("pool_step")
        norms_summed = sem("norms_summed")
        norms_rooted = sem("norms_rooted")
        rot_ready = sem("rot_ready")
        gb_ready = sem("gb_ready")
        w_hi_ready = sem("w_hi_ready")
        ms_ready = sem("ms_ready")
        inv_ready = sem("inv_ready")
        xs_ready = sem("xs_ready")
        xn_hi_ready = sem("xn_hi_ready")
        xn_lo_ready = sem("xn_lo_ready")
        part1_ready = sem("part1_ready")
        part2_ready = sem("part2_ready")
        parts_ready = sem("parts_ready")
        parts_saved = [sem(f"parts_saved{j}") for j in range(4)]
        stack_loaded = [sem(f"stack_loaded{i}") for i in range(SLOTS)]
        max_loaded = [sem(f"max_loaded{i}") for i in range(NHALF * SLOTS)]
        nmax_saved = sem("nmax_saved")
        max_filled = sem("max_filled")
        max_used = sem("max_used")
        nmax_split = sem("nmax_split")
        ones_loaded = sem("ones_loaded")
        o_cleared = sem("o_cleared")
        scores_filled = sem("scores_filled")
        exp_done = sem("exp_done")
        pv_done = sem("pv_done")
        o_copied = sem("o_copied")
        at_hi_ready = sem("at_hi_ready")
        squares_done = sem("squares_done")
        x12_ready = sem("x12_ready")
        ys_ready = sem("ys_ready")
        yn_hi_ready = sem("yn_hi_ready")
        yn_lo_ready = sem("yn_lo_ready")
        h_hi_ready = sem("h_hi_ready")
        h_lo_ready = sem("h_lo_ready")
        h_used = sem("h_used")
        stored = sem("stored")

        def wait_filled(eng, *key):
            eng.wait_ge(tile_filled, plan[key][0] + 1)

        def wait_evacuated(eng, *key):
            eng.wait_ge(evacuated[plan[key][1]], plan[key][2])

        def wait_bank(eng, *key):
            if before[key]:
                eng.wait_ge(evacuated[plan[key][1]], before[key])

        def bank_of(*key):
            return psum[:, plan[key][1], :]

        def free_sem(*key):
            return evacuated[plan[key][1]]

        def max_slot(item):
            s = 2 * (max_no[item] % 2)
            return psum[:, s:s + 2, :]

        def e_bank(e):
            return psum[:, 4 + e % EB, :]

        O_BANK = psum[:, 7, :]
        def gb_col(b, norm, off, kt):
            i = 4 * norm + 2 * off + kt
            return gb[:, b, i:i + 1]

        def wait_h_used(eng, n):
            c, ht = ffn_units[n]
            if ht == HT - 1:
                wait_filled(eng, "out", c, CT - 1)
            else:
                eng.wait_ge(h_used, c * (HT - 1) + ht + 1)

        def wait_item(eng, *item):
            eng.wait_ge(max_used, max_no[item] + 1)

        def fw_dst(n, part):
            r, i = n // 2, n % 2
            if r < 4:
                w, half = r // 2, r % 2
                return (fw_hi, fw_lo)[part][:, w, i, half * 512:half * 512 + 512]
            ht = 4 * (r - 4) + 2 * i
            return (fo_hi, fo_lo)[part][:, ht:ht + 2, :].rearrange("p a d -> p (a d)")

        def wait_preparation(eng):
            wait_filled(eng, "V", NCH - 1, 1)
            eng.wait_ge(parts_ready, 4 * NCH)
            for j in range(4):
                eng.wait_ge(parts_saved[j], 16 * NCH)

        block = ctx.enter_context(nc.Block())

        @block.sync
        def _(sp):
            for half in range(2):
                cols = slice(half * QUAT, (half + 1) * QUAT)
                sp.dma_start(par_rows[0:4, cols], q_right).then_inc(par_loaded, 16)
                sp.dma_start(par_rows[4:6, cols], cond).then_inc(par_loaded, 16)
                sp.dma_start(par_rows[6:7, cols], gate[0, 0]).then_inc(par_loaded, 16)
            for w, bias in enumerate((g1b, b1b, g2b, b2b)):
                sp.dma_start(par_rows[7 + 2 * w:9 + 2 * w, :],
                             bias.rearrange("(k p) -> k p", p=P)).then_inc(par_loaded, 16)

            def load_x(c):
                sp.dma_start(x_in[c % 2][:, :, :],
                             x[c // BCH, (c % BCH) * CW:(c % BCH + 1) * CW, :].rearrange("(t p) d -> p t d", p=P)
                             ).then_inc(x_loaded[c], 16)

            load_x(1)
            sp.dma_start(cond_bc[:, :, :], cond.partition_broadcast(P)).then_inc(cond_loaded, 16)
            for w, weight in enumerate((g1w, b1w, g2w, b2w)):
                sp.dma_start(gw[:, 2 * w:2 * w + 2, :],
                             weight.rearrange("(k p) d -> p k d", p=P)).then_inc(cond_loaded, 16)
            sp.wait_ge(consts_ready, 5)
            for i in range(SLOTS):
                sp.dma_start(k_st[i][PROD_ROWS:ALL_ROWS, :, :],
                             ones_row[:, :].unsqueeze(1).to_broadcast([3, GH, SEQ])).then_inc(ones_loaded, 16)

            def save_parts(c):
                for j in range(4):
                    sp.wait_ge(parts_ready, 4 * c + j + 1)
                    ch = (j % 2) * P
                    sp.dma_start(scr_qk[j // 2, :, ch:ch + P, c * CW:(c + 1) * CW].rearrange("a p t -> p a t"),
                                 qk_parts[j][:, :, :]).then_inc(parts_saved[j], 16)

            def load_stack(g):
                b, hg = g // (NG // BATCH), g % (NG // BATCH)
                if g >= SLOTS:
                    sp.wait_ge(pv_done, (g - SLOTS + 1) * NHALF * LT)
                for j in range(4):
                    sp.wait_ge(parts_saved[j], 16 * BCH * (b + 1))
                ch, tok = slice(hg * GH * DH, (hg + 1) * GH * DH), slice(b * SEQ, (b + 1) * SEQ)
                row = 0
                for part, times in Q_PARTS:
                    for _ in range(times):
                        sp.dma_start(q_st[g % SLOTS][row:row + DH, :, :],
                                     scr_qk[0, part, ch, tok].rearrange("(h d) t -> d h t", d=DH)
                                     ).then_inc(stack_loaded[g % SLOTS], 16)
                        row += DH
                for i, part in enumerate(K_PARTS):
                    sp.dma_start(k_st[g % SLOTS][i * DH:(i + 1) * DH, :, :],
                                 scr_qk[1, part, ch, tok].rearrange("(h d) t -> d h t", d=DH)
                                 ).then_inc(stack_loaded[g % SLOTS], 16)

            def load_max(n):
                slot, half = n // NHALF % SLOTS, n % NHALF
                sp.wait_ge(max_used, max_no["T", n] + 1)
                sp.dma_start(scr_max[n].rearrange("a (q l) -> (a q) l", l=P), nmax_t[:, :]).then_inc(nmax_saved, 16)
                sp.wait_ge(nmax_saved, 16 * (n + 1))
                sp.dma_start(q_st[slot][PROD_ROWS:ALL_ROWS, :, half * HALF:(half + 1) * HALF],
                             scr_max[n].rearrange("a (h l) -> a h l", h=GH)
                             ).then_inc(max_loaded[NHALF * slot + half], 16)

            for c in range(2, NCH):
                wait_filled(sp, "x_T", c - 2, 1)
                load_x(c)
            for c in range(BCH):
                save_parts(c)
            load_stack(0)
            save_parts(BCH)
            load_stack(1)
            load_max(0)
            save_parts(BCH + 1)
            load_stack(2)
            for g in range(1, NG):
                if SLOTS <= g + 1 < NG:
                    load_stack(g + 1)
                load_max(NHALF * g - 1)
                load_max(NHALF * g)
            load_max(NHALF * NG - 1)
            for c in range(NCH):
                for tt in range(CT):
                    wait_evacuated(sp, "out", c, tt)
                sp.dma_start(out[c // BCH, (c % BCH) * CW:(c % BCH + 1) * CW, :].rearrange("(t p) d -> p t d", p=P),
                             attn[:, c * CT:(c + 1) * CT, :]).then_inc(stored, 16)
            sp.wait_ge(stored, 16 * NCH)

        @block.gpsimd
        def _(pool):
            nc.gpsimd.memset(neg_half[:, :], -0.5).then_inc(pool_step, 1)
            nc.gpsimd.memset(ident[:, :], 0.0).then_inc(pool_step, 1)
            pool.wait_ge(pool_step, 2)
            nc.gpsimd.affine_select(out=ident[:, :], in_=ident[:, :], compare_op=ALU.not_equal, fill=1.0, base=0,
                                    pattern=[[-1, P]], channel_multiplier=1).then_inc(consts_ready, 1)
            pool.wait_ge(consts_ready, 1)
            nc.gpsimd.tensor_tensor(diag64[:, :], ident[:, 0:QUAT], ident[:, QUAT:P], ALU.add).then_inc(consts_ready, 1)
            nc.gpsimd.tensor_copy(ident_bf[:, :], ident[:, :]).then_inc(consts_ready, 1)
            pool.wait_ge(norms_summed, 1)
            nc.gpsimd.tensor_tensor(small[:, 10:12], small[:, 6:8], neg_half[:, 0:2], ALU.pow).then_inc(norms_rooted, 1)
            nc.gpsimd.memset(v_sb[:, :, :, DH:VW], 1.0).then_inc(consts_ready, 1)
            pool.wait_ge(consts_ready, 4)
            nc.gpsimd.memset(ones_row[:, :], 1.0).then_inc(consts_ready, 1)
            pool.wait_ge(consts_ready, 5)

            def low_part(c):
                for kt in range(KT):
                    pool.wait_ge(xn_hi_ready, KT * c + kt + 1)
                    nc.gpsimd.tensor_tensor(xn_lo[c % 2][:, kt, :], xf[:, kt, :],
                                            xn_hi[c % 2][:, kt, :].bitcast(f32), ALU.subtract
                                            ).then_inc(xn_lo_ready, 1)

            def inverse_root(norm, c):
                pool.wait_ge(ms_ready, NCH * norm + c + 1)
                t = slice(c * CT, (c + 1) * CT)
                nc.gpsimd.tensor_tensor(inv_rms[:, norm, t], ms[:, norm, t], neg_half[:, :], ALU.pow
                                        ).then_inc(inv_ready, 1)

            def third_part(c, j):
                n = 4 * c + j
                pool.wait_ge(part2_ready, n + 1)
                nc.gpsimd.tensor_tensor(qk_parts[j][:, 2, :], qk_rest[n % 3][:, :], qk_parts[j][:, 1, :],
                                        ALU.subtract).then_inc(parts_ready, 1)

            def add_residuals(c):
                t = slice(c * CT, (c + 1) * CT)
                nc.gpsimd.tensor_tensor(x1[:, t, :], x1[:, t, :], attn[:, t, :], ALU.add).then_inc(x12_ready, 1)

            def low_part2(c, kt):
                pool.wait_ge(yn_hi_ready, KT * c + kt + 1)
                nc.gpsimd.tensor_tensor(yn_lo[c][:, kt, :], yn_f[:, kt, :], yn_hi[c][:, kt, :].bitcast(f32),
                                        ALU.subtract).then_inc(yn_lo_ready, 1)

            for step in prep:
                if step[0] == "SC":
                    inverse_root(0, step[1])
                elif step[0] == "xs_T" and step[1] >= BCH:
                    low_part(step[1])
                elif step[0] == "QK":
                    third_part(step[1], step[2])
            for c in range(BCH):
                inverse_root(1, c)
                for pair in range(2):
                    wait_item(pool, "WO", c, pair)
                pool.wait_ge(squares_done, NT + CT * (c + 1))
                add_residuals(c)
                for kt in range(KT):
                    low_part2(c, kt)
            for step in fin:
                if step[0] == "SC":
                    inverse_root(1, step[1])
                elif step[0] == "WO" and step[2] == 1:
                    c = step[1]
                    for pair in range(2):
                        wait_evacuated(pool, "WO", c, pair)
                    add_residuals(c)
                elif step[0] == "y_T":
                    low_part2(step[1], step[2])
                elif step[0] == "F" and 1 <= step[1] <= len(ffn_units):
                    n = step[1] - 1
                    pool.wait_ge(h_hi_ready, n + 1)
                    nc.gpsimd.tensor_tensor(h_lo[n % 3][:, :], h_f[n % 2][:, :], h_hi[n % 3][:, :].bitcast(f32),
                                            ALU.subtract).then_inc(h_lo_ready, 1)

        @block.scalar
        def _(act):
            act.dma_start(x_in[0][:, :, :], x[0, 0:CW, :].rearrange("(t p) d -> p t d", p=P)).then_inc(x_loaded[0], 16)
            for i, w in enumerate((wq, wk, wv, wo)):
                act.dma_start(w_raw[:, i, :, :], w.rearrange("(t p) d -> p t d", p=P)).then_inc(w_loaded, 16)

            def copy_x_t(c):
                for kt in range(KT):
                    wait_filled(act, "x_T", c, kt)
                    if c >= 2 and kt == 0:
                        wait_filled(act, "L0", c - 2, 1)
                    nc.scalar.activation(x_t[c % 2][:, kt, :], bank_of("x_T", c, kt), ACT.Copy
                                         ).then_inc(free_sem("x_T", c, kt), 1)

            def sum_squares(norm, t, src):
                n = norm * NT + t
                if n >= 2:
                    act.wait_ge(squares_done, n - 1)
                nc.scalar.activation(squares[:, n % 2, :], src, ACT.Square, accum_out=sumsq[:, norm, t:t + 1]
                                     ).then_inc(squares_done, 1)

            def copy_x1(c):
                for pair in range(2):
                    t = c * CT + 2 * pair
                    src = bank_of("L0", c, pair).rearrange("p (t d) -> p t d", t=2)
                    wait_filled(act, "L0", c, pair)
                    for i in range(2):
                        sum_squares(0, t + i, src[:, i, :])
                    nc.scalar.activation(x1[:, t:t + 2, :], src, ACT.Copy).then_inc(free_sem("L0", c, pair), 1)

            def norm_affine(norm, c, kt):
                b = c // BCH
                key = ("y_T" if norm else "xs_T", c, kt)
                act.wait_ge(gb_ready, 1)
                if c:
                    act.wait_ge(yn_lo_ready if norm else xn_lo_ready, KT * (c - 1) + kt + 1)
                wait_filled(act, *key)
                nc.scalar.activation((yn_f if norm else xf)[:, kt, :], bank_of(*key), ACT.Identity,
                                     scale=gb_col(b, norm, 0, kt), bias=gb_col(b, norm, 1, kt)
                                     ).then_inc(free_sem(*key), 1)

            def part1(c, j):
                wait_filled(act, "QK", c, j)
                if c:
                    act.wait_ge(parts_saved[j], 16 * c)
                nc.scalar.activation(qk_parts[j][:, 0, :], bank_of("QK", c, j), ACT.Copy,
                                     scale=DH ** -0.5 if j < 2 else 1.0).then_inc(part1_ready, 1)

            def part2(n):
                c, j = n // 4, n % 4
                wait_evacuated(act, "QK", c, j)
                nc.scalar.activation(qk_parts[j][:, 1, :], qk_rest[n % 3][:, :], ACT.Copy).then_inc(part2_ready, 1)

            for step in prep:
                what, rest = step[0], step[1:]
                if what == "x_T":
                    copy_x_t(*rest)
                elif what == "W":
                    for i in range(4):
                        wait_filled(act, "W", i)
                        dst = w_hi[:, i, :, :] if i < 3 else wo_hi[:, :, :]
                        nc.scalar.activation(dst, bank_of("W", i).rearrange("p (k d) -> p k d", k=KT), ACT.Copy
                                             ).then_inc(w_hi_ready, 1)
                elif what == "L0":
                    copy_x1(*rest)
                elif what == "xs_T":
                    for kt in range(KT):
                        norm_affine(0, *rest, kt)
                elif what == "QK":
                    part1(*rest)
                    if rest[1]:
                        part2(4 * rest[0] + rest[1] - 1)
                elif what == "V":
                    c, pair = rest
                    if pair == 0:
                        part2(4 * c + 3)
                    if c == 0:
                        act.wait_ge(consts_ready, 4)
                    t = c * CT + 2 * pair
                    wait_filled(act, "V", c, pair)
                    nc.scalar.activation(v_sb[:, t:t + 2, :, 0:DH],
                                         bank_of("V", c, pair).rearrange("p (t h d) -> p t h d", t=2, d=DH),
                                         ACT.Copy).then_inc(free_sem("V", c, pair), 1)

            wait_preparation(act)
            for s in range(NSTEP + 1):
                if s < NSTEP:
                    for h in range(GH):
                        e = GH * s + h
                        act.wait_ge(scores_filled, e + 1)
                        if s >= PR // GH and h == 0:
                            act.wait_ge(pv_done, s - PR // GH + 1)
                        nc.scalar.activation(prob[e % PR][:, :], e_bank(e), ACT.Exp).then_inc(exp_done, 1)
                if s and s % LT == 0:
                    o = s // LT - 1
                    act.wait_ge(pv_done, s)
                    if o:
                        act.wait_ge(max_filled, max_no["O", o - 1] + 1)
                    nc.scalar.activation(ot[:, :], O_BANK, ACT.Copy).then_inc(o_copied, 1)

                if s in square_steps:
                    c, pair = square_steps[s]
                    wait_item(act, "WO", c, pair)
                    for i in range(2):
                        sum_squares(1, c * CT + 2 * pair + i, attn[:, c * CT + 2 * pair + i, :])
                if s in fw_loads:
                    r = fw_loads[s]
                    if r:
                        act.wait_ge(max_filled, max_no["FW", 2 * r - 1] + 1)
                    if r < 4:
                        src = (gate_w, hid_w)[r // 2][(r % 2) * 512:(r % 2 + 1) * 512, :]
                        act.dma_start(f_raw[:, :, :], src.rearrange("(t p) d -> p t d", p=P)).then_inc(f_loaded, 16)
                    else:
                        act.dma_start(f_raw[:, :, :].rearrange("p a d -> p (a d)").rearrange("p (t n) -> p t n", t=KT),
                                      out_w[:, (r - 4) * 512:(r - 3) * 512].rearrange("(t p) n -> p t n", p=P)
                                      ).then_inc(f_loaded, 16)

            def high_hidden(n):
                wait_evacuated(act, "hid", n)
                if n >= 3:
                    wait_h_used(act, n - 3)
                nc.scalar.activation(h_hi[n % 3][:, :], h_f[n % 2][:, :], ACT.Copy).then_inc(h_hi_ready, 1)

            for step in fin:
                what, rest = step[0], step[1:]
                if what == "a_T":
                    c, kt = rest
                    wait_filled(act, "a_T", c, kt)
                    nc.scalar.activation(at_hi[:, kt, :], bank_of("a_T", c, kt), ACT.Copy).then_inc(at_hi_ready, 1)
                elif what == "WO":
                    c, pair = rest
                    wait_evacuated(act, "WO", c, pair)
                    for i in range(2):
                        sum_squares(1, c * CT + 2 * pair + i, attn[:, c * CT + 2 * pair + i, :])
                elif what == "y_T":
                    norm_affine(1, *rest)
                elif what == "F":
                    n = rest[0]
                    if n < len(ffn_units):
                        wait_filled(act, "gate", n)
                        if n >= 2:
                            wait_evacuated(act, "hid", n - 2)
                        nc.scalar.activation(silu_g[n % 2][:, :], bank_of("gate", n), ACT.Silu
                                             ).then_inc(free_sem("gate", n), 1)
                    if 1 <= n <= len(ffn_units):
                        high_hidden(n - 1)

        @block.vector
        def _(dve):
            steps = [0]

            def link(ins):
                steps[0] += 1
                ins.then_inc(vector_step, 1)
                dve.wait_ge(vector_step, steps[0])

            wait_filled(dve, "par")
            nc.vector.tensor_copy(qc[:, :], bank_of("par")[:, 0:15]).then_inc(free_sem("par"), 1)
            wait_evacuated(dve, "par")
            link(nc.vector.tensor_tensor(small[:, 0:6], qc[:, 0:6], qc[:, 0:6], ALU.mult))
            nc.vector.reduce_sum(small[:, 6:7], small[:, 0:4], AX.X)
            link(nc.vector.reduce_sum(small[:, 7:8], small[:, 4:6], AX.X))
            nc.vector.tensor_scalar_add(small[:, 6:8], small[:, 6:8], QEPS).then_inc(norms_summed, 1)
            dve.wait_ge(norms_rooted, 1)
            link(nc.vector.tensor_scalar(small[:, 12:16], qc[:, 0:4], small[:, 10:11], qc[:, 6:7], ALU.mult, ALU.mult))
            nc.vector.tensor_scalar(small[:, 16:20], small[:, 12:16], -1.0, None, ALU.mult)
            link(nc.vector.tensor_scalar(small[:, 20:22], qc[:, 4:6], small[:, 11:12], None, ALU.mult))
            right = small[:, 24:32].rearrange("p (t k) -> p t k", t=KT)
            signed = ((0, 5, 6, 7), (1, 0, 3, 6), (2, 7, 0, 1), (3, 2, 5, 0))
            for j, row in enumerate(signed):
                part = slice(QUAT * (j % 2), QUAT * (j % 2) + QUAT)
                for k, i in enumerate(row):
                    last = nc.vector.tensor_copy(right[part, j // 2, k:k + 1], small[part, 12 + i:13 + i])
            link(last)
            tmp = small[:, 32:40].rearrange("p (t k) -> p t k", t=KT)
            cross = small[:, 40:48].rearrange("p (t k) -> p t k", t=KT)

            def r(k):
                return right[:, :, k:k + 1]

            for k, (a, b, op) in enumerate(((1, 2, ALU.add), (3, 2, ALU.subtract), (1, 3, ALU.subtract),
                                            (2, 1, ALU.subtract))):
                last = nc.vector.tensor_tensor(tmp[:, :, k:k + 1], r(a), r(b), op)
            link(last)
            nc.vector.scalar_tensor_tensor(out=cross[:, :, 0:1], in0=tmp[:, :, 0:1], scalar=-1.0, in1=r(3),
                                           op0=ALU.mult, op1=ALU.subtract)
            link(nc.vector.tensor_tensor(cross[:, :, 1:4], tmp[:, :, 1:4], r(0).to_broadcast([P, KT, 3]), ALU.add))
            link(nc.vector.tensor_scalar(small[:, 48:56], small[:, 40:48], small[:, 21:22], None, ALU.mult))
            link(nc.vector.scalar_tensor_tensor(out=small[:, 56:64], in0=small[:, 24:32], scalar=small[:, 20:21],
                                                in1=small[:, 48:56], op0=ALU.mult, op1=ALU.add))
            dve.wait_ge(consts_ready, 2)
            rot_blocks = rot[:, :, :].rearrange("p t (k c) -> p (t k) c", c=QUAT)
            link(nc.vector.tensor_tensor(rot_blocks, diag64[:, :].unsqueeze(1).to_broadcast([P, 8, QUAT]),
                                         small[:, 56:64].unsqueeze(2).to_broadcast([P, 8, QUAT]), ALU.mult))
            for kt in range(KT):
                diag = rot[:, kt, kt * P:(kt + 1) * P]
                last = nc.vector.tensor_tensor(diag, diag, ident[:, :], ALU.add)
            last.then_inc(rot_ready, 1)

            dve.wait_ge(cond_loaded, 16 * 5)
            for b in range(BATCH):
                link(nc.vector.tensor_tensor(gprod[:, :, :], gw[:, :, :],
                                             cond_bc[:, b:b + 1, :].to_broadcast([P, 8, DT]), ALU.mult))
                link(nc.vector.reduce_sum(gb[:, b, :], gprod[:, :, :], AX.X))
                last = nc.vector.tensor_tensor(gb[:, b, :], gb[:, b, :], qc[:, 7:15], ALU.add)
            last.then_inc(gb_ready, 1)

            def mean_squares(norm, c):
                t = slice(c * CT, (c + 1) * CT)
                nc.vector.tensor_scalar(ms[:, norm, t], sumsq[:, norm, t], 1.0 / D, NEPS, ALU.mult, ALU.add
                                        ).then_inc(ms_ready, 1)

            def scale_tokens(norm, c, src, dst, ready):
                dve.wait_ge(inv_ready, NCH * norm + c + 1)
                for i in range(CT):
                    n = c * CT + i
                    last = nc.vector.tensor_scalar(dst[:, i, :], src[:, n, :], inv_rms[:, norm, n:n + 1], None,
                                                   ALU.mult)
                last.then_inc(ready, 1)

            def item_of_max_slot(item):
                what, n = item[0], item[1]
                slot = max_slot(item)
                dve.wait_ge(max_filled, max_no[item] + 1)
                if what == "max":
                    b, h, t = n // HU % 2, n % HU // HT_Q, n % HT_Q
                    nc.vector.tensor_reduce(out=nmax[:, b, h, t:t + 1], in_=slot, axis=AX.XY, op=ALU.max,
                                            negate=True).then_inc(max_used, 1)
                    if n % HU == HU - 1:
                        all_max = nmax[:, b, :, :].rearrange("p h t -> p (h t)")
                        dve.wait_ge(max_used, max_no[item] + 1)
                        link(nc.vector.tensor_copy(nmax_parts[:, 0, :], all_max))
                        link(nc.vector.tensor_tensor(nmax_rest[:, :], all_max, nmax_parts[:, 0, :], ALU.subtract))
                        link(nc.vector.tensor_copy(nmax_parts[:, 1, :], nmax_rest[:, :]))
                        nc.vector.tensor_tensor(nmax_parts[:, 2, :], nmax_rest[:, :], nmax_parts[:, 1, :],
                                                ALU.subtract).then_inc(nmax_split, 1)
                elif what == "T":
                    if n:
                        dve.wait_ge(nmax_saved, 16 * n)
                    nc.vector.tensor_copy(nmax_t[:, :], slot[0:3 * HU, 0, 0:P // 2].bitcast(bf16)).then_inc(max_used, 1)
                elif what == "O":
                    o = slot[:, 0, :].rearrange("p (t h d) -> p t h d", t=CT, h=GH)
                    g, half = n // NHALF, n % NHALF
                    b, hg = g // (NG // BATCH), g % (NG // BATCH)
                    t = b * LT + half * CT
                    if n:
                        wait_item(dve, "O", n - 1)
                    link(nc.vector.reciprocal(rsum[:, :, :, :], o[:, :, :, DH:VW]))
                    nc.vector.tensor_tensor(
                        attn[:, t:t + CT, hg * GH * DH:(hg + 1) * GH * DH].rearrange("p t (h d) -> p t h d", d=DH),
                        o[:, :, :, 0:DH], rsum[:, :, :, :].to_broadcast([P, CT, GH, DH]), ALU.mult
                    ).then_inc(max_used, 1)
                elif what == "a_T":
                    kt = item[2]
                    link(nc.vector.tensor_copy(at_hi[:, kt, :], slot[:, 0, :]))
                    nc.vector.tensor_tensor(at_lo[:, kt, :], slot[:, 0, :], at_hi[:, kt, :].bitcast(f32), ALU.subtract
                                            ).then_inc(max_used, 1)
                elif what == "FW":
                    link(nc.vector.tensor_copy(fw_dst(n, 0), slot[:, 0, :]))
                    nc.vector.tensor_tensor(fw_dst(n, 1), slot[:, 0, :], fw_dst(n, 0).bitcast(f32), ALU.subtract
                                            ).then_inc(max_used, 1)
                elif what == "WO":
                    t = n * CT + 2 * item[2]
                    nc.vector.tensor_tensor(attn[:, t:t + 2, :], slot[:, 0, :].rearrange("p (t d) -> p t d", t=2),
                                            x1[:, t:t + 2, :], ALU.add).then_inc(max_used, 1)
                else:
                    kt = item[2]
                    if n:
                        dve.wait_ge(yn_lo_ready, KT * (n - 1) + kt + 1)
                    nc.vector.tensor_scalar(yn_f[:, kt, :], slot[:, 0, :], gb_col(n // BCH, 1, 0, kt),
                                            gb_col(n // BCH, 1, 1, kt), ALU.mult, ALU.add).then_inc(max_used, 1)
                    wait_item(dve, *item)
                    nc.vector.tensor_copy(yn_hi[n][:, kt, :], yn_f[:, kt, :]).then_inc(yn_hi_ready, 1)

            for step in prep:
                what, rest = step[0], step[1:]
                if what == "W":
                    for i in range(4):
                        dve.wait_ge(w_hi_ready, i + 1)
                        hi, lo = (w_hi[:, i, :, :], w_lo[:, i, :, :]) if i < 3 else (wo_hi[:, :, :], wo_lo[:, :, :])
                        nc.vector.tensor_tensor(lo, bank_of("W", i).rearrange("p (k d) -> p k d", k=KT),
                                                hi.bitcast(f32), ALU.subtract).then_inc(free_sem("W", i), 1)
                elif what == "SC":
                    c = rest[0]
                    for pair in range(2):
                        wait_evacuated(dve, "L0", c, pair)
                    mean_squares(0, c)
                    if c >= 2:
                        wait_filled(dve, "xs_T", c - 2, 1)
                    scale_tokens(0, c, x1, xs[c % 2], xs_ready)
                elif what == "xs_T":
                    c = rest[0]
                    if c >= 2:
                        wait_filled(dve, "V", c - 2, 1)
                    for kt in range(KT):
                        wait_evacuated(dve, "xs_T", c, kt)
                        nc.vector.tensor_copy(xn_hi[c % 2][:, kt, :], xf[:, kt, :]).then_inc(xn_hi_ready, 1)
                        if c < BCH:
                            dve.wait_ge(xn_hi_ready, KT * c + kt + 1)
                            nc.vector.tensor_tensor(xn_lo[c % 2][:, kt, :], xf[:, kt, :],
                                                    xn_hi[c % 2][:, kt, :].bitcast(f32), ALU.subtract
                                                    ).then_inc(xn_lo_ready, 1)
                elif what == "QK":
                    c, j = rest
                    n = 4 * c + j
                    dve.wait_ge(part1_ready, n + 1)
                    if n >= 3:
                        dve.wait_ge(parts_ready, n - 2)
                    nc.vector.scalar_tensor_tensor(out=qk_rest[n % 3][:, :], in0=bank_of("QK", c, j),
                                                   scalar=DH ** -0.5 if j < 2 else 1.0,
                                                   in1=qk_parts[j][:, 0, :], op0=ALU.mult, op1=ALU.subtract
                                                   ).then_inc(free_sem("QK", c, j), 1)
                elif what == "item":
                    item_of_max_slot(rest[0])

            if prep_total[7]:
                dve.wait_ge(evacuated[7], prep_total[7])
            nc.vector.memset(O_BANK, 0.0).then_inc(o_cleared, 1)
            wait_preparation(dve)
            for s in range(NSTEP + 2):
                for item in max_items(s):
                    item_of_max_slot(item)
                if s in mean_steps:
                    c = mean_steps[s]
                    dve.wait_ge(squares_done, NT + CT * (c + 1))
                    mean_squares(1, c)
                if s in scale_steps:
                    scale_tokens(1, scale_steps[s], attn, xs2, ys_ready)

            for step in fin:
                what, rest = step[0], step[1:]
                if what == "a_T":
                    c, kt = rest
                    dve.wait_ge(at_hi_ready, KT * (c - BCH) + kt + 1)
                    nc.vector.tensor_tensor(at_lo[:, kt, :], bank_of("a_T", c, kt), at_hi[:, kt, :].bitcast(f32),
                                            ALU.subtract).then_inc(free_sem("a_T", c, kt), 1)
                    continue
                if what == "WO":
                    c, pair = rest
                    t = c * CT + 2 * pair
                    wait_filled(dve, "WO", c, pair)
                    nc.vector.tensor_tensor(attn[:, t:t + 2, :], bank_of("WO", c, pair).rearrange("p (t d) -> p t d", t=2),
                                            x1[:, t:t + 2, :], ALU.add).then_inc(free_sem("WO", c, pair), 1)
                    continue
                if what == "SC":
                    c = rest[0]
                    dve.wait_ge(squares_done, NT + CT * (c + 1))
                    mean_squares(1, c)
                    scale_tokens(1, c, attn, xs2, ys_ready)
                    continue
                if what == "y_T":
                    c, kt = rest
                    wait_evacuated(dve, "y_T", c, kt)
                    nc.vector.tensor_copy(yn_hi[c][:, kt, :], yn_f[:, kt, :]).then_inc(yn_hi_ready, 1)
                    continue
                n = rest[0]
                if n < len(ffn_units):
                    wait_evacuated(dve, "gate", n)
                    wait_filled(dve, "hid", n)
                    if n >= 2:
                        dve.wait_ge(h_lo_ready, n - 1)
                    nc.vector.tensor_tensor(h_f[n % 2][:, :], bank_of("hid", n), silu_g[n % 2][:, :], ALU.mult
                                            ).then_inc(free_sem("hid", n), 1)
                if n >= OUT_LAG and ffn_units[n - OUT_LAG][1] == HT - 1:
                    c = ffn_units[n - OUT_LAG][0]
                    dve.wait_ge(x12_ready, c + 1)
                    for tt in range(CT):
                        wait_filled(dve, "out", c, tt)
                        nc.vector.tensor_tensor(attn[:, c * CT + tt, :], bank_of("out", c, tt)[:, 0:D],
                                                x1[:, c * CT + tt, :], ALU.add).then_inc(free_sem("out", c, tt), 1)

        @block.tensor
        def _(pe):
            def blocks(dst, srcs):
                for i, src in enumerate(srcs):
                    last = nc.tensor.transpose(dst[:, i * P:(i + 1) * P], src, ident[:, :])
                return last

            def transposes(key, srcs):
                wait_bank(pe, *key)
                blocks(bank_of(*key), srcs).then_inc(tile_filled, 1)

            def a_blocks(c, kt):
                return [attn[:, c * CT + t, kt * P:(kt + 1) * P] for t in range(CT)]

            def y_blocks(kt):
                return [xs2[:, t, kt * P:(kt + 1) * P] for t in range(CT)]

            def project_out(dst, pair):
                for i in range(2):
                    t = slice((2 * pair + i) * P, (2 * pair + i + 1) * P)
                    last = split_product(dst[:, i * D:(i + 1) * D],
                                         [(at_hi[:, kt, t], at_lo[:, kt, t]) for kt in range(KT)],
                                         [(wo_hi[:, kt, :], wo_lo[:, kt, :]) for kt in range(KT)])
                return last

            def split_product(dst, stationary, moving, first=True, last=True):
                passes = [(s, m) for (sh, sl), (mh, ml) in zip(stationary, moving)
                          for s, m in ((sl, mh), (sh, ml), (sh, mh))]
                for i, (s, m) in enumerate(passes):
                    ins = nc.tensor.matmul(dst, s, m, start=first and i == 0, stop=last and i == len(passes) - 1)
                return ins

            pe.wait_ge(consts_ready, 1)
            pe.wait_ge(par_loaded, 16 * 10)
            nc.tensor.transpose(bank_of("par")[:, 0:15], par_rows[:, :], ident[0:15, 0:15]).then_inc(tile_filled, 1)

            def qkv_ready(c):
                if c == 0:
                    for i in range(3):
                        wait_evacuated(pe, "W", i)
                for kt in range(KT):
                    wait_evacuated(pe, "xs_T", c, kt)
                pe.wait_ge(xn_lo_ready, KT * (c + 1))

            def operands_loaded(g):
                pe.wait_ge(stack_loaded[g % SLOTS], 16 * 2 * len(K_PARTS) * (g // SLOTS + 1))

            def do_item(item):
                what, n = item[0], item[1]
                slot = max_slot(item)
                if max_no[item] >= 2:
                    pe.wait_ge(max_used, max_no[item] - 1)
                else:
                    for i in range(4):
                        pe.wait_ge(evacuated[i], before_items[i])
                    pe.wait_ge(consts_ready, 3)
                if what == "max":
                    g, h, lt = unit(n)
                    if n % GU == 0:
                        operands_loaded(g)
                    for half in range(SEQ // 512):
                        last = nc.tensor.matmul(slot[:, half, :], q_st[g % SLOTS][0:PROD_ROWS, h, lt * P:(lt + 1) * P],
                                                k_st[g % SLOTS][0:PROD_ROWS, h, half * 512:(half + 1) * 512],
                                                start=True, stop=True)
                elif what == "T":
                    pe.wait_ge(nmax_split, n + 1)
                    last = nc.tensor.transpose(slot[0:3 * HU, 0, 0:P // 2].bitcast(bf16),
                                               nmax_parts[:, :, :].rearrange("p a q -> p (a q)"), ident_bf[:, :])
                elif what == "O":
                    pe.wait_ge(o_copied, n + 1)
                    last = blocks(slot[:, 0, :], [ot[:, t * P:(t + 1) * P] for t in range(CT)])
                elif what == "a_T":
                    last = blocks(slot[:, 0, :], a_blocks(n, item[2]))
                elif what == "WO":
                    wait_item(pe, "a_T", n, 1)
                    last = project_out(slot[:, 0, :], item[2])
                elif what == "y_T":
                    pe.wait_ge(ys_ready, n + 1)
                    last = blocks(slot[:, 0, :], y_blocks(item[2]))
                else:
                    r, i = n // 2, n % 2
                    pe.wait_ge(f_loaded, 16 * (r + 1))
                    if r < 4:
                        srcs = [f_raw[:, t, i * P:(i + 1) * P] for t in range(CT)]
                    else:
                        raw = f_raw[:, :, :].rearrange("p a d -> p (a d)").rearrange("p (t n) -> p t n", t=KT)
                        srcs = [raw[:, t, (2 * i + a) * P:(2 * i + a + 1) * P] for a in range(2) for t in range(KT)]
                    last = blocks(slot[:, 0, :], srcs)
                last.then_inc(max_filled, 1)

            def scores(s, h):
                g, half, kt = s // (NHALF * LT), s // LT % NHALF, s % LT
                e = GH * s + h
                if e >= EB:
                    pe.wait_ge(exp_done, e - EB + 1)
                if s % LT == 0 and h == 0:
                    pe.wait_ge(max_loaded[NHALF * (g % SLOTS) + half], 16 * (g // SLOTS + 1))
                nc.tensor.matmul(e_bank(e), k_st[g % SLOTS][0:ALL_ROWS, h, kt * P:(kt + 1) * P],
                                 q_st[g % SLOTS][0:ALL_ROWS, h, half * HALF:(half + 1) * HALF],
                                 start=True, stop=True).then_inc(scores_filled, 1)

            def values(s):
                g, kt = s // (NHALF * LT), s % LT
                b, hg = g // (NG // BATCH), g % (NG // BATCH)
                pe.wait_ge(exp_done, GH * (s + 1))
                if kt == 0:
                    if s:
                        pe.wait_ge(o_copied, s // LT)
                    else:
                        pe.wait_ge(o_cleared, 1)
                for h in range(GH):
                    last = nc.tensor.matmul(O_BANK[32 * h:32 * h + VW, :], v_sb[:, b * LT + kt, hg * GH + h, :],
                                            prob[(GH * s + h) % PR][:, :], start=kt == 0, stop=kt == LT - 1)
                last.then_inc(pv_done, 1)

            for step in prep:
                what, rest = step[0], step[1:]
                if what == "x_T":
                    c = rest[0]
                    pe.wait_ge(x_loaded[c], 16)
                    for kt in range(KT):
                        transposes(("x_T", c, kt), [x_in[c % 2][:, t, kt * P:(kt + 1) * P] for t in range(CT)])
                elif what == "W":
                    pe.wait_ge(w_loaded, 16 * 4)
                    for i in range(4):
                        transposes(("W", i), [w_raw[:, i, t, kt * P:(kt + 1) * P]
                                              for kt in range(KT) for t in range(KT)])
                elif what == "L0":
                    c = rest[0]
                    if c == 0:
                        pe.wait_ge(rot_ready, 1)
                    for kt in range(KT):
                        wait_evacuated(pe, "x_T", c, kt)
                    for pair in range(2):
                        wait_bank(pe, "L0", c, pair)
                        for i in range(2):
                            t = 2 * pair + i
                            for kt in range(KT):
                                last = nc.tensor.matmul(bank_of("L0", c, pair)[:, i * D:(i + 1) * D],
                                                        x_t[c % 2][:, kt, t * P:(t + 1) * P], rot[:, kt, :],
                                                        start=kt == 0, stop=kt == KT - 1)
                        last.then_inc(tile_filled, 1)
                elif what == "xs_T":
                    c = rest[0]
                    pe.wait_ge(xs_ready, c + 1)
                    for kt in range(KT):
                        transposes(("xs_T", c, kt), [xs[c % 2][:, t, kt * P:(kt + 1) * P] for t in range(CT)])
                elif what == "QK":
                    c, j = rest
                    if j == 0:
                        qkv_ready(c)
                    hi, lo = xn_hi[c % 2], xn_lo[c % 2]
                    cols = slice((j % 2) * P, (j % 2 + 1) * P)
                    wait_bank(pe, "QK", c, j)
                    split_product(bank_of("QK", c, j),
                                  [(w_hi[:, j // 2, kt, cols], w_lo[:, j // 2, kt, cols]) for kt in range(KT)],
                                  [(hi[:, kt, :], lo[:, kt, :]) for kt in range(KT)]).then_inc(tile_filled, 1)
                elif what == "V":
                    c, pair = rest
                    hi, lo = xn_hi[c % 2], xn_lo[c % 2]
                    wait_bank(pe, "V", c, pair)
                    for i in range(2):
                        t = slice((2 * pair + i) * P, (2 * pair + i + 1) * P)
                        last = split_product(bank_of("V", c, pair)[:, i * D:(i + 1) * D],
                                             [(hi[:, kt, t], lo[:, kt, t]) for kt in range(KT)],
                                             [(w_hi[:, 2, kt, :], w_lo[:, 2, kt, :]) for kt in range(KT)])
                    last.then_inc(tile_filled, 1)
                elif what == "item":
                    do_item(rest[0])

            for i in range(4, 8):
                pe.wait_ge(evacuated[i], prep_total[i])
            pe.wait_ge(ones_loaded, 16 * SLOTS)
            for s in range(NSTEP + 2):
                if s < NSTEP:
                    for h in range(GH - 1):
                        scores(s, h)
                items = max_items(s)
                early = 1 if items and items[0][0] == "max" else 0
                for item in items[:early]:
                    do_item(item)
                if 1 <= s <= NSTEP:
                    values(s - 1)
                if s < NSTEP:
                    scores(s, GH - 1)
                for item in items[early:]:
                    do_item(item)

            pe.wait_ge(max_used, len(max_no))
            pe.wait_ge(exp_done, GH * NSTEP)
            pe.wait_ge(o_copied, NG * NHALF)
            for step in fin:
                what, rest = step[0], step[1:]
                if what == "a_T":
                    transposes(("a_T", *rest), a_blocks(*rest))
                    continue
                if what == "WO":
                    c, pair = rest
                    for kt in range(KT):
                        wait_evacuated(pe, "a_T", c, kt)
                    wait_bank(pe, "WO", c, pair)
                    project_out(bank_of("WO", c, pair), pair).then_inc(tile_filled, 1)
                    continue
                if what == "y_T":
                    c, kt = rest
                    pe.wait_ge(ys_ready, c + 1)
                    transposes(("y_T", c, kt), y_blocks(kt))
                    continue
                if what != "F":
                    continue
                n = rest[0]
                if n < len(ffn_units):
                    c, ht = ffn_units[n]
                    if ht == 0:
                        pe.wait_ge(yn_lo_ready, KT * (c + 1))
                    cols = slice(ht * P, (ht + 1) * P)
                    for w, name in enumerate(("gate", "hid")):
                        wait_bank(pe, name, n)
                        split_product(bank_of(name, n),
                                      [(fw_hi[:, w, kt, cols], fw_lo[:, w, kt, cols]) for kt in range(KT)],
                                      [(yn_hi[c][:, kt, :], yn_lo[c][:, kt, :]) for kt in range(KT)]
                                      ).then_inc(tile_filled, 1)
                if n >= OUT_LAG:
                    m = n - OUT_LAG
                    c, ht = ffn_units[m]
                    pe.wait_ge(h_lo_ready, m + 1)
                    for tt in range(CT):
                        if ht == 0:
                            wait_bank(pe, "out", c, tt)
                        t = slice(tt * P, (tt + 1) * P)
                        ins = split_product(bank_of("out", c, tt)[:, 0:D], [(h_hi[m % 3][:, t], h_lo[m % 3][:, t])],
                                            [(fo_hi[:, ht, :], fo_lo[:, ht, :])], ht == 0, ht == HT - 1)
                        if ht == HT - 1:
                            ins.then_inc(tile_filled, 1)
                    if ht < HT - 1:
                        ins.then_inc(h_used, 1)


NAMES = ["x", "cond_256", "L0_cond_q_right", "L0_cond_spectral_gate", "L1_cond_Wq", "L1_cond_Wk", "L1_cond_Wv",
         "L1_cond_Wo", "L1_cond_g1w", "L1_cond_g1b", "L1_cond_b1w", "L1_cond_b1b", "L1_cond_g2w", "L1_cond_g2b",
         "L1_cond_b2w", "L1_cond_b2b", "L1_cond_gate_w", "L1_cond_hid_w", "L1_cond_out_w"]


def kernel(**inputs):
    import numpy as _np
    import concourse.bacc as _bacc
    from concourse import mybir as _mybir
    from concourse.bass_utils import run_bass_kernel_spmd as _run

    nc = _bacc.Bacc("TRN2", target_bir_lowering=False, num_devices=1)
    arrays, args = {}, []
    for name in NAMES:
        a = _np.ascontiguousarray(inputs[name])
        arrays[f"in_{name}"] = a
        args.append(nc.dram_tensor(f"in_{name}", a.shape, _mybir.dt.from_np(a.dtype), kind="ExternalInput").ap())
    args.append(nc.dram_tensor("out_x", (BATCH, SEQ, D), _mybir.dt.float32, kind="ExternalOutput").ap())
    build(nc, *args)
    r = _run(nc, [arrays], core_ids=[0])
    return r.results[0]["out_x"]
```

```python
import concourse.bass as bass
from concourse import mybir
from contextlib import ExitStack

P = 128
BATCH, SEQ, D = 2, 1024, 256
HEADS, DH = 16, 16
HIDDEN = 1024
QUAT = D // 4
DT = 64
TOK = BATCH * SEQ
NT = TOK // P
CT = 4
CW = CT * P
NCH = NT // CT
BCH = NCH // BATCH
KT = D // P
GH = 4
NG = BATCH * HEADS // GH
LT = SEQ // P
HALF = 512
NHALF = SEQ // HALF
HT_Q = HALF // P
VW = DH + 1
Q_PARTS = ((0, 3), (1, 2), (2, 1))
K_PARTS = (0, 1, 2, 0, 1, 0)
PROD_ROWS = DH * len(K_PARTS)
ALL_ROWS = PROD_ROWS + 3
SLOTS = 3
EB = 3
PR = 8
LEAD = 12
HT = HIDDEN // P
DVE_CHUNKS = 3
QEPS, NEPS = 1e-8, 1e-6


def build(nc, x, cond, q_right, gate, wq, wk, wv, wo, g1w, g1b, b1w, b1b, g2w, g2b, b2w, b2b,
          gate_w, hid_w, out_w, out):
    f32, f32r, bf16 = mybir.dt.float32, mybir.dt.float32r, mybir.dt.bfloat16
    ALU, ACT, AX = mybir.AluOpType, mybir.ActivationFunctionType, mybir.AxisListType

    ctx = ExitStack()
    with ctx:
        def sb(name, shape, dt, scope=None):
            return (scope or ctx).enter_context(nc.sbuf_tensor(name, shape, dt))

        def sem(name):
            return ctx.enter_context(nc.semaphore(name))

        ident = sb("ident", [P, P], f32)
        ident_bf = sb("ident_bf", [P, P], bf16)
        x1 = sb("x1", [P, NT, D], f32)
        attn = sb("attn", [P, NT, D], f32)
        wo_hi, wo_lo = (sb(f"wo_{s}", [P, KT, D], f32r) for s in ("hi", "lo"))
        gb = sb("gb", [P, BATCH, 8], f32)
        sumsq = sb("sumsq", [P, 2, NT], f32)
        ms = sb("ms", [P, 2, NT], f32)
        inv_rms = sb("inv_rms", [P, 2, NT], f32)
        neg_half = sb("neg_half", [P, CT], f32)
        qc = sb("qc", [P, 15], f32)
        squares = sb("squares", [P, 2, D], bf16)

        nmax = sb("nmax", [P, 2, GH, HT_Q], f32)
        nmax_rest = sb("nmax_rest", [P, GH * HT_Q], f32)
        nmax_parts = sb("nmax_parts", [P, 3, GH * HT_Q], bf16)
        nmax_t = sb("nmax_t", [3 * GH * HT_Q, P], bf16)
        rsum = sb("rsum", [P, CT, GH, 1], f32)

        scope_b = ExitStack()
        v_sb = sb("v_sb", [P, NT, HEADS, VW], f32, scope_b)
        q_st = [sb(f"q_st{i}", [P, GH, SEQ], bf16, scope_b) for i in range(SLOTS)]
        k_st = [sb(f"k_st{i}", [P, GH, SEQ], bf16, scope_b) for i in range(SLOTS)]

        scope_p = ExitStack()
        par_rows = sb("par_rows", [7, QUAT], f32, scope_p)
        par_twice = sb("par_twice", [7, P], f32, scope_p)
        bias_rows = sb("bias_rows", [8, P], f32, scope_p)
        cond_bc = sb("cond_bc", [P, BATCH, DT], f32, scope_p)
        gw = sb("gw", [P, 8, DT], f32, scope_p)
        gprod = sb("gprod", [P, 8, DT], f32, scope_p)
        diag64 = sb("diag64", [P, QUAT], f32, scope_p)
        small = sb("small", [P, 64], f32, scope_p)
        rot = sb("rot", [P, KT, D], f32, scope_p)
        w_raw = sb("w_raw", [P, 4, KT, D], f32, scope_p)
        w_hi = sb("w_hi", [P, 3, KT, D], f32r, scope_p)
        w_lo = sb("w_lo", [P, 3, KT, D], f32r, scope_p)
        ones_row = sb("ones_row", [3, SEQ], bf16, scope_p)
        x_in = [sb(f"x_in{i}", [P, CT, D], f32, scope_p) for i in range(2)]
        x_t = [sb(f"x_t{i}", [P, KT, CW], f32, scope_p) for i in range(2)]
        xs = [sb(f"xs{i}", [P, CT, D], f32, scope_p) for i in range(2)]
        xf = sb("xf", [P, KT, CW], f32, scope_p)
        xn_hi = [sb(f"xn_hi{i}", [P, KT, CW], f32r, scope_p) for i in range(2)]
        xn_lo = [sb(f"xn_lo{i}", [P, KT, CW], f32r, scope_p) for i in range(2)]
        qk_rest = [sb(f"qk_rest{i}", [P, CW], f32, scope_p) for i in range(3)]
        qk_parts = [sb(f"qk_parts{i}", [P, 3, CW], bf16, scope_p) for i in range(4)]
        scope_p.close()

        prob = [sb(f"prob{i}", [P, HALF], f32, scope_b) for i in range(PR)]
        ot = sb("ot", [P, HALF], f32, scope_b)
        f_raw = sb("f_raw", [P, 4, D], f32, scope_b)
        fw_hi = sb("fw_hi", [P, 2, KT, HIDDEN], f32r, scope_b)
        fw_lo = sb("fw_lo", [P, 2, KT, HIDDEN], f32r, scope_b)
        fo_hi = sb("fo_hi", [P, HT, D], f32r, scope_b)
        fo_lo = sb("fo_lo", [P, HT, D], f32r, scope_b)
        at_hi = sb("at_hi", [P, KT, CW], f32r, scope_b)
        at_lo = sb("at_lo", [P, KT, CW], f32r, scope_b)
        xs2 = sb("xs2", [P, CT, D], f32, scope_b)
        yn_f = sb("yn_f", [P, KT, CW], f32, scope_b)
        yn_hi = [sb(f"yn_hi{i}", [P, KT, CW], f32r, scope_b) for i in range(BCH)]
        yn_lo = [sb(f"yn_lo{i}", [P, KT, CW], f32r, scope_b) for i in range(BCH)]
        scope_b.close()
        yn_hi += [sb(f"yn_hi{i}", [P, KT, CW], f32r) for i in range(BCH, NCH)]
        yn_lo += [sb(f"yn_lo{i}", [P, KT, CW], f32r) for i in range(BCH, NCH)]
        silu_g = [sb(f"silu_g{i}", [P, CW], f32) for i in range(2)]
        h_f = [sb(f"h_f{i}", [P, CW], f32) for i in range(2)]
        h_hi = [sb(f"h_hi{i}", [P, CW], f32r) for i in range(3)]
        h_lo = [sb(f"h_lo{i}", [P, CW], f32r) for i in range(3)]

        psum = ctx.enter_context(nc.psum_tensor("psum", [P, 8, 512], f32))
        scr_qk = nc.dram_tensor("scr_qk", (2, 3, D, TOK), bf16, kind="Internal").ap()
        scr_max = nc.dram_tensor("scr_max", (NG * NHALF, 3, GH * HALF), bf16, kind="Internal").ap()

        plan, bank_total = {}, [0] * 8
        before = {}

        def plan_tile(key, bank):
            before[key] = bank_total[bank]
            bank_total[bank] += 1
            plan[key] = (len(plan), bank, bank_total[bank])

        def qkv(c):
            return [("QK", c, j) for j in range(4)] + [("V", c, pair) for pair in range(2)]

        NSTEP = NG * NHALF * LT
        UNITS = NG * GH * LT
        GU = GH * LT
        HU = GH * HT_Q
        T_AT = 4
        first_items = ([("max", u) for u in range(HU + T_AT)] + [("T", 0)]
                       + [("max", u) for u in range(HU + T_AT, HU + LEAD)])

        def unit(u):
            half, h, t = u % GU // HU, u % HU // HT_Q, u % HT_Q
            return u // GU, h, half * HT_Q + t

        half_done = NSTEP // BATCH
        placed = {half_done + d: item for d, item in (
            (-6, ("a_T", 0, 0)), (-3, ("a_T", 0, 1)), (-1, ("WO", 0, 0)), (2, ("WO", 0, 1)),
            (5, ("a_T", 1, 0)), (7, ("a_T", 1, 1)), (10, ("WO", 1, 0)), (13, ("WO", 1, 1)),
            (15, ("y_T", 0, 0)), (18, ("y_T", 0, 1)), (23, ("y_T", 1, 0)), (26, ("y_T", 1, 1)))}
        fw_steps = [half_done + d for d in (31, 32, 37, 38, 43, 45, 50, 51, 55, 56, 60, 61)]
        placed |= {step: ("FW", n) for n, step in enumerate(fw_steps)}
        fw_loads = {half_done + 24: 0} | {fw_steps[2 * r - 1] + 1: r for r in range(1, 6)}
        square_steps = {half_done + 1: (0, 0), half_done + 4: (0, 1), half_done + 12: (1, 0), half_done + 15: (1, 1)}
        mean_steps = {half_done + 6: 0, half_done + 17: 1}

        cuts = [placed[step] for step in sorted(placed) if placed[step][0] != "WO"]
        cut_no = {item: i for i, item in enumerate(cuts)}

        def max_items(step):
            items = []
            if step % LT == 1 and step > LT:
                items.append(("O", step // LT - 1))
            if step in placed:
                items.append(placed[step])
            first = HU + LEAD + 2 * step
            if first % HU == T_AT and first // HU - 1 < NG * NHALF:
                items.append(("T", first // HU - 1))
            if first >= UNITS:
                return items
            return [("max", first)] + items + [("max", first + 1)]

        last_output = ("O", NG * NHALF - 1)
        max_no = {}
        for item in first_items + [i for step in range(NSTEP) for i in max_items(step)] + [last_output]:
            max_no[item] = len(max_no)

        EARLY = 3
        prep = [("x_T", 0), ("bias",), ("W",), ("L0", 0), ("SC", 0), ("x_T", 1), ("L0", 1), ("SC", 1), ("xs_T", 0)]
        prep += [("x_T", 2), ("L0", 2), ("xs_T", 1)] + qkv(0) + [("SC", 2)] + qkv(1)
        prep += [("switch",), ("xs_T", 2), ("x_T", 3), ("L0", 3)]
        tail, pending = qkv(2)[:2] + [("xs_T", 3)] + qkv(2)[2:] + qkv(3), list(first_items)
        prep += [("item", it) for it in pending[:EARLY]] + [("SC", 3)]
        pending = pending[EARLY:]
        for i, what in enumerate(tail):
            prep.append(what)
            take = -(-len(pending) // (len(tail) - i))
            prep += [("item", it) for it in pending[:take]]
            pending = pending[take:]

        ring, width = [0], [8]
        plan_tile(("par",), 7)

        def plan_ring(key):
            plan_tile(key, 8 - width[0] + ring[0] % width[0])
            ring[0] += 1

        before_items = [0] * 8
        for step in prep:
            if step[0] == "switch":
                before_items = list(bank_total)
                width[0], ring[0] = 4, 0
            elif step[0] == "bias":
                plan_ring(step)
            elif step[0] == "W":
                for i in range(4):
                    plan_ring(("W", i))
            elif step[0] in ("x_T", "L0", "xs_T"):
                for i in range(2):
                    plan_ring((*step, i))
            elif step[0] in ("QK", "V"):
                plan_ring(step)
        prep_total = list(bank_total)

        OUT_LAG = 2
        ffn_units = [(c, ht) for c in range(NCH) for ht in range(HT)]
        fin = ([("F", 0), last_output, ("a_T", 2, 0), ("a_T", 2, 1), ("F", 1), ("WO", 2, 0), ("WO", 2, 1), ("F", 2),
                ("a_T", 3, 0), ("a_T", 3, 1), ("SC", 2), ("F", 3), ("WO", 3, 0), ("WO", 3, 1), ("F", 4),
                ("y_T", 2, 0), ("y_T", 2, 1), ("F", 5), ("SC", 3), ("F", 6), ("y_T", 3, 0), ("y_T", 3, 1)]
               + [("F", n) for n in range(7, len(ffn_units) + OUT_LAG)])
        ring[0] = 0
        for step in fin:
            if step[0] == "F":
                n = step[1]
                if n < len(ffn_units):
                    plan_ring(("gate", n))
                    plan_ring(("hid", n))
                if n >= OUT_LAG and ffn_units[n - OUT_LAG][1] == HT - 1:
                    for tt in range(CT):
                        plan_tile(("out", ffn_units[n - OUT_LAG][0], tt), tt)
            elif step[0] not in ("SC", "O"):
                plan_ring(step)

        par_loaded = sem("par_loaded")
        par_doubled = sem("par_doubled")
        bias_loaded = sem("bias_loaded")
        cond_loaded = sem("cond_loaded")
        w_loaded = sem("w_loaded")
        x_loaded = [sem(f"x_loaded{c}") for c in range(NCH)]
        f_loaded = sem("f_loaded")
        consts_ready = sem("consts_ready")
        tile_filled = sem("tile_filled")
        evacuated = [sem(f"evacuated{i}") for i in range(8)]
        vector_step = sem("vector_step")
        pool_step = sem("pool_step")
        norms_summed = sem("norms_summed")
        norms_rooted = sem("norms_rooted")
        rot_ready = sem("rot_ready")
        gb_ready = sem("gb_ready")
        w_hi_ready = sem("w_hi_ready")
        ms_ready = sem("ms_ready")
        inv_ready = sem("inv_ready")
        xs_ready = sem("xs_ready")
        xn_hi_ready = sem("xn_hi_ready")
        xn_lo_ready = sem("xn_lo_ready")
        part1_ready = sem("part1_ready")
        part2_ready = sem("part2_ready")
        parts_ready = sem("parts_ready")
        parts_saved = [sem(f"parts_saved{j}") for j in range(4)]
        stack_loaded = [sem(f"stack_loaded{i}") for i in range(SLOTS)]
        max_loaded = [sem(f"max_loaded{i}") for i in range(NHALF * SLOTS)]
        nmax_saved = sem("nmax_saved")
        max_filled = sem("max_filled")
        max_used = sem("max_used")
        parts_step = sem("parts_step")
        nmax_split = sem("nmax_split")
        ones_loaded = sem("ones_loaded")
        o_cleared = sem("o_cleared")
        scores_filled = sem("scores_filled")
        exp_done = sem("exp_done")
        pv_done = sem("pv_done")
        o_copied = sem("o_copied")
        at_hi_ready = sem("at_hi_ready")
        squares_done = sem("squares_done")
        x12_ready = sem("x12_ready")
        ys_ready = sem("ys_ready")
        yn_hi_ready = sem("yn_hi_ready")
        cut_hi_ready = sem("cut_hi_ready")
        cut_ready = sem("cut_ready")
        yn_lo_ready = sem("yn_lo_ready")
        h_hi_ready = sem("h_hi_ready")
        h_lo_ready = sem("h_lo_ready")
        h_used = sem("h_used")
        stored = sem("stored")

        def wait_filled(eng, *key):
            eng.wait_ge(tile_filled, plan[key][0] + 1)

        def wait_evacuated(eng, *key):
            eng.wait_ge(evacuated[plan[key][1]], plan[key][2])

        def wait_bank(eng, *key):
            if before[key]:
                eng.wait_ge(evacuated[plan[key][1]], before[key])

        def bank_of(*key):
            return psum[:, plan[key][1], :]

        def free_sem(*key):
            return evacuated[plan[key][1]]

        def max_slot(item):
            s = 2 * (max_no[item] % 2)
            return psum[:, s:s + 2, :]

        def e_bank(e):
            return psum[:, 4 + e % EB, :]

        O_BANK = psum[:, 7, :]
        def gb_col(b, norm, off, kt):
            i = 4 * norm + 2 * off + kt
            return gb[:, b, i:i + 1]

        def wait_h_used(eng, n):
            c, ht = ffn_units[n]
            if ht == HT - 1:
                wait_filled(eng, "out", c, CT - 1)
            else:
                eng.wait_ge(h_used, c * (HT - 1) + ht + 1)

        def wait_item(eng, *item):
            eng.wait_ge(max_used, max_no[item] + 1)

        def fw_dst(n, part):
            r, i = n // 2, n % 2
            if r < 4:
                w, half = r // 2, r % 2
                return (fw_hi, fw_lo)[part][:, w, i, half * 512:half * 512 + 512]
            ht = 4 * (r - 4) + 2 * i
            return (fo_hi, fo_lo)[part][:, ht:ht + 2, :].rearrange("p a d -> p (a d)")

        def wait_cut(eng, *item):
            eng.wait_ge(cut_ready, cut_no[item] + 1)

        def cut_dst(item, part):
            if item[0] == "FW":
                return fw_dst(item[1], part)
            hi_lo = (at_hi, at_lo) if item[0] == "a_T" else (yn_hi[item[1]], yn_lo[item[1]])
            return hi_lo[part][:, item[2], :]

        def wait_preparation(eng):
            wait_filled(eng, "V", NCH - 1, 1)
            eng.wait_ge(parts_ready, 4 * NCH)
            for j in range(4):
                eng.wait_ge(parts_saved[j], 16 * NCH)

        block = ctx.enter_context(nc.Block())

        @block.sync
        def _(sp):
            sp.dma_start(par_rows[0:4, :], q_right).then_inc(par_loaded, 16)
            sp.dma_start(par_rows[4:6, :], cond).then_inc(par_loaded, 16)
            sp.dma_start(par_rows[6:7, :], gate[0, 0]).then_inc(par_loaded, 16)
            for w, bias in enumerate((g1b, b1b, g2b, b2b)):
                sp.dma_start(bias_rows[2 * w:2 * w + 2, :],
                             bias.rearrange("(k p) -> k p", p=P)).then_inc(bias_loaded, 16)

            def load_x(c):
                sp.dma_start(x_in[c % 2][:, :, :],
                             x[c // BCH, (c % BCH) * CW:(c % BCH + 1) * CW, :].rearrange("(t p) d -> p t d", p=P)
                             ).then_inc(x_loaded[c], 16)

            load_x(1)
            sp.dma_start(cond_bc[:, :, :], cond.partition_broadcast(P)).then_inc(cond_loaded, 16)
            for w, weight in enumerate((g1w, b1w, g2w, b2w)):
                sp.dma_start(gw[:, 2 * w:2 * w + 2, :],
                             weight.rearrange("(k p) d -> p k d", p=P)).then_inc(cond_loaded, 16)
            sp.wait_ge(consts_ready, 5)
            for i in range(SLOTS):
                sp.dma_start(k_st[i][PROD_ROWS:ALL_ROWS, :, :],
                             ones_row[:, :].unsqueeze(1).to_broadcast([3, GH, SEQ])).then_inc(ones_loaded, 16)

            def save_parts(c, tiles=range(4)):
                for j in tiles:
                    sp.wait_ge(parts_ready, 4 * c + j + 1)
                    ch = (j // 2) * P
                    sp.dma_start(scr_qk[j % 2, :, ch:ch + P, c * CW:(c + 1) * CW].rearrange("a p t -> p a t"),
                                 qk_parts[j][:, :, :]).then_inc(parts_saved[j], 16)

            def load_stack(g):
                b, hg = g // (NG // BATCH), g % (NG // BATCH)
                if g >= SLOTS:
                    sp.wait_ge(pv_done, (g - SLOTS + 1) * NHALF * LT)
                for j in (hg // 2 * 2, hg // 2 * 2 + 1):
                    sp.wait_ge(parts_saved[j], 16 * BCH * (b + 1))
                ch, tok = slice(hg * GH * DH, (hg + 1) * GH * DH), slice(b * SEQ, (b + 1) * SEQ)
                row = 0
                for part, times in Q_PARTS:
                    for _ in range(times):
                        sp.dma_start(q_st[g % SLOTS][row:row + DH, :, :],
                                     scr_qk[0, part, ch, tok].rearrange("(h d) t -> d h t", d=DH)
                                     ).then_inc(stack_loaded[g % SLOTS], 16)
                        row += DH
                for i, part in enumerate(K_PARTS):
                    sp.dma_start(k_st[g % SLOTS][i * DH:(i + 1) * DH, :, :],
                                 scr_qk[1, part, ch, tok].rearrange("(h d) t -> d h t", d=DH)
                                 ).then_inc(stack_loaded[g % SLOTS], 16)

            def load_max(n):
                slot, half = n // NHALF % SLOTS, n % NHALF
                sp.wait_ge(max_used, max_no["T", n] + 1)
                sp.dma_start(scr_max[n].rearrange("a (q l) -> (a q) l", l=P), nmax_t[:, :]).then_inc(nmax_saved, 16)
                sp.wait_ge(nmax_saved, 16 * (n + 1))
                sp.dma_start(q_st[slot][PROD_ROWS:ALL_ROWS, :, half * HALF:(half + 1) * HALF],
                             scr_max[n].rearrange("a (h l) -> a h l", h=GH)
                             ).then_inc(max_loaded[NHALF * slot + half], 16)

            for c in range(2, NCH):
                wait_filled(sp, "x_T", c - 2, 1)
                load_x(c)
            save_parts(0)
            save_parts(1, (0, 1))
            load_stack(0)
            save_parts(1, (2, 3))
            save_parts(BCH)
            load_stack(1)
            load_max(0)
            save_parts(BCH + 1)
            load_stack(2)
            for g in range(1, NG):
                if SLOTS <= g + 1 < NG:
                    load_stack(g + 1)
                load_max(NHALF * g - 1)
                load_max(NHALF * g)
            load_max(NHALF * NG - 1)
            for c in range(NCH):
                for tt in range(CT):
                    wait_evacuated(sp, "out", c, tt)
                sp.dma_start(out[c // BCH, (c % BCH) * CW:(c % BCH + 1) * CW, :].rearrange("(t p) d -> p t d", p=P),
                             attn[:, c * CT:(c + 1) * CT, :]).then_inc(stored, 16)
            sp.wait_ge(stored, 16 * NCH)

        @block.gpsimd
        def _(pool):
            nc.gpsimd.memset(neg_half[:, :], -0.5).then_inc(pool_step, 1)
            nc.gpsimd.memset(ident[:, :], 0.0).then_inc(pool_step, 1)
            pool.wait_ge(pool_step, 2)
            nc.gpsimd.affine_select(out=ident[:, :], in_=ident[:, :], compare_op=ALU.not_equal, fill=1.0, base=0,
                                    pattern=[[-1, P]], channel_multiplier=1).then_inc(consts_ready, 1)
            pool.wait_ge(consts_ready, 1)
            nc.gpsimd.tensor_tensor(diag64[:, :], ident[:, 0:QUAT], ident[:, QUAT:P], ALU.add).then_inc(consts_ready, 1)
            nc.gpsimd.tensor_copy(ident_bf[:, :], ident[:, :]).then_inc(consts_ready, 1)
            pool.wait_ge(norms_summed, 1)
            nc.gpsimd.tensor_tensor(small[:, 10:12], small[:, 6:8], neg_half[:, 0:2], ALU.pow).then_inc(norms_rooted, 1)
            nc.gpsimd.memset(v_sb[:, :, :, DH:VW], 1.0).then_inc(consts_ready, 1)
            pool.wait_ge(consts_ready, 4)
            nc.gpsimd.memset(ones_row[:, :], 1.0).then_inc(consts_ready, 1)
            pool.wait_ge(consts_ready, 5)

            def low_part(c):
                for kt in range(KT):
                    pool.wait_ge(xn_hi_ready, KT * c + kt + 1)
                    nc.gpsimd.tensor_tensor(xn_lo[c % 2][:, kt, :], xf[:, kt, :],
                                            xn_hi[c % 2][:, kt, :].bitcast(f32), ALU.subtract
                                            ).then_inc(xn_lo_ready, 1)

            def inverse_root(norm, c):
                pool.wait_ge(ms_ready, NCH * norm + c + 1)
                t = slice(c * CT, (c + 1) * CT)
                nc.gpsimd.tensor_tensor(inv_rms[:, norm, t], ms[:, norm, t], neg_half[:, :], ALU.pow
                                        ).then_inc(inv_ready, 1)

            def third_part(c, j):
                n = 4 * c + j
                pool.wait_ge(part2_ready, n + 1)
                nc.gpsimd.tensor_tensor(qk_parts[j][:, 2, :], qk_rest[n % 3][:, :], qk_parts[j][:, 1, :],
                                        ALU.subtract).then_inc(parts_ready, 1)

            def add_residuals(c):
                t = slice(c * CT, (c + 1) * CT)
                nc.gpsimd.tensor_tensor(x1[:, t, :], x1[:, t, :], attn[:, t, :], ALU.add).then_inc(x12_ready, 1)

            def low_part2(c, kt):
                pool.wait_ge(yn_hi_ready, KT * (c - BCH) + kt + 1)
                nc.gpsimd.tensor_tensor(yn_lo[c][:, kt, :], yn_f[:, kt, :], yn_hi[c][:, kt, :].bitcast(f32),
                                        ALU.subtract).then_inc(yn_lo_ready, 1)

            for step in prep:
                if step[0] == "SC":
                    inverse_root(0, step[1])
                elif step[0] == "xs_T" and step[1] >= DVE_CHUNKS:
                    low_part(step[1])
                elif step[0] == "QK":
                    third_part(step[1], step[2])
            for step in sorted(set(mean_steps) | set(placed)):
                if step in mean_steps:
                    c = mean_steps[step]
                    inverse_root(1, c)
                    pool.wait_ge(inv_ready, NCH + c + 1)
                    t = slice(c * CT, (c + 1) * CT)
                    if c:
                        wait_item(pool, "y_T", c - 1, 1)
                    nc.gpsimd.tensor_tensor(xs2[:, :, :], attn[:, t, :],
                                            inv_rms[:, 1, t].unsqueeze(2).to_broadcast([P, CT, D]), ALU.mult
                                            ).then_inc(ys_ready, 1)
                    pool.wait_ge(ys_ready, c + 1)
                    add_residuals(c)
                    pool.wait_ge(x12_ready, c + 1)
                item = placed.get(step)
                if item in cut_no:
                    n = cut_no[item]
                    wait_item(pool, *item)
                    nc.gpsimd.tensor_copy(cut_dst(item, 0), yn_f[:, n % 2, :]).then_inc(cut_hi_ready, 1)
                    pool.wait_ge(cut_hi_ready, n + 1)
                    nc.gpsimd.tensor_tensor(cut_dst(item, 1), yn_f[:, n % 2, :], cut_dst(item, 0).bitcast(f32),
                                            ALU.subtract).then_inc(cut_ready, 1)
            for step in fin:
                if step[0] == "SC":
                    inverse_root(1, step[1])
                elif step[0] == "WO" and step[2] == 1:
                    c = step[1]
                    for pair in range(2):
                        wait_evacuated(pool, "WO", c, pair)
                    add_residuals(c)
                elif step[0] == "y_T":
                    low_part2(step[1], step[2])
                elif step[0] == "F" and 1 <= step[1] <= len(ffn_units):
                    n = step[1] - 1
                    pool.wait_ge(h_hi_ready, n + 1)
                    nc.gpsimd.tensor_tensor(h_lo[n % 3][:, :], h_f[n % 2][:, :], h_hi[n % 3][:, :].bitcast(f32),
                                            ALU.subtract).then_inc(h_lo_ready, 1)

        @block.scalar
        def _(act):
            act.dma_start(x_in[0][:, :, :], x[0, 0:CW, :].rearrange("(t p) d -> p t d", p=P)).then_inc(x_loaded[0], 16)
            for i, w in enumerate((wq, wk, wv, wo)):
                act.dma_start(w_raw[:, i, :, :], w.rearrange("(t p) d -> p t d", p=P)).then_inc(w_loaded, 16)

            def copy_x_t(c):
                for kt in range(KT):
                    wait_filled(act, "x_T", c, kt)
                    if c >= 2 and kt == 0:
                        wait_filled(act, "L0", c - 2, 1)
                    nc.scalar.activation(x_t[c % 2][:, kt, :], bank_of("x_T", c, kt), ACT.Copy
                                         ).then_inc(free_sem("x_T", c, kt), 1)

            def sum_squares(norm, t, src):
                n = norm * NT + t
                if n >= 2:
                    act.wait_ge(squares_done, n - 1)
                nc.scalar.activation(squares[:, n % 2, :], src, ACT.Square, accum_out=sumsq[:, norm, t:t + 1]
                                     ).then_inc(squares_done, 1)

            def copy_x1(c):
                for pair in range(2):
                    t = c * CT + 2 * pair
                    src = bank_of("L0", c, pair).rearrange("p (t d) -> p t d", t=2)
                    wait_filled(act, "L0", c, pair)
                    for i in range(2):
                        sum_squares(0, t + i, src[:, i, :])
                    nc.scalar.activation(x1[:, t:t + 2, :], src, ACT.Copy).then_inc(free_sem("L0", c, pair), 1)

            def norm_affine(norm, c, kt):
                b = c // BCH
                key = ("y_T" if norm else "xs_T", c, kt)
                act.wait_ge(gb_ready, 1)
                if norm and c == BCH:
                    act.wait_ge(cut_ready, len(cuts))
                elif norm:
                    act.wait_ge(yn_lo_ready, KT * (c - BCH - 1) + kt + 1)
                elif c:
                    act.wait_ge(xn_lo_ready, KT * (c - 1) + kt + 1)
                wait_filled(act, *key)
                nc.scalar.activation((yn_f if norm else xf)[:, kt, :], bank_of(*key), ACT.Identity,
                                     scale=gb_col(b, norm, 0, kt), bias=gb_col(b, norm, 1, kt)
                                     ).then_inc(free_sem(*key), 1)

            def part1(c, j):
                wait_filled(act, "QK", c, j)
                if c:
                    act.wait_ge(parts_saved[j], 16 * c)
                nc.scalar.activation(qk_parts[j][:, 0, :], bank_of("QK", c, j), ACT.Copy,
                                     scale=1.0 if j % 2 else DH ** -0.5).then_inc(part1_ready, 1)

            def part2(n):
                c, j = n // 4, n % 4
                wait_evacuated(act, "QK", c, j)
                nc.scalar.activation(qk_parts[j][:, 1, :], qk_rest[n % 3][:, :], ACT.Copy).then_inc(part2_ready, 1)

            for step in prep:
                what, rest = step[0], step[1:]
                if what == "x_T":
                    copy_x_t(*rest)
                elif what == "W":
                    for i in range(4):
                        wait_filled(act, "W", i)
                        dst = w_hi[:, i, :, :] if i < 3 else wo_hi[:, :, :]
                        nc.scalar.activation(dst, bank_of("W", i).rearrange("p (k d) -> p k d", k=KT), ACT.Copy
                                             ).then_inc(w_hi_ready, 1)
                elif what == "L0":
                    copy_x1(*rest)
                elif what == "SC" and rest[0] >= DVE_CHUNKS:
                    c = rest[0]
                    act.wait_ge(inv_ready, c + 1)
                    wait_filled(act, "xs_T", c - 2, 1)
                    for i in range(CT):
                        n = c * CT + i
                        last = nc.scalar.activation(xs[c % 2][:, i, :], x1[:, n, :], ACT.Copy,
                                                    scale=inv_rms[:, 0, n:n + 1])
                    last.then_inc(xs_ready, 1)
                elif what == "xs_T":
                    c = rest[0]
                    for kt in range(KT):
                        norm_affine(0, c, kt)
                    if c >= DVE_CHUNKS:
                        wait_filled(act, "V", c - 2, 1)
                        for kt in range(KT):
                            wait_evacuated(act, "xs_T", c, kt)
                            nc.scalar.activation(xn_hi[c % 2][:, kt, :], xf[:, kt, :], ACT.Copy
                                                 ).then_inc(xn_hi_ready, 1)
                elif what == "QK":
                    part1(*rest)
                    if rest[1]:
                        part2(4 * rest[0] + rest[1] - 1)
                elif what == "V":
                    c, pair = rest
                    if pair == 0:
                        part2(4 * c + 3)
                    if c == 0:
                        act.wait_ge(consts_ready, 4)
                    t = c * CT + 2 * pair
                    wait_filled(act, "V", c, pair)
                    nc.scalar.activation(v_sb[:, t:t + 2, :, 0:DH],
                                         bank_of("V", c, pair).rearrange("p (t h d) -> p t h d", t=2, d=DH),
                                         ACT.Copy).then_inc(free_sem("V", c, pair), 1)

            wait_preparation(act)
            for s in range(NSTEP + 1):
                if s < NSTEP:
                    for h in range(GH):
                        e = GH * s + h
                        act.wait_ge(scores_filled, e + 1)
                        if s >= PR // GH and h == 0:
                            act.wait_ge(pv_done, s - PR // GH + 1)
                        nc.scalar.activation(prob[e % PR][:, :], e_bank(e), ACT.Exp).then_inc(exp_done, 1)
                if s and s % LT == 0:
                    o = s // LT - 1
                    act.wait_ge(pv_done, s)
                    if o:
                        act.wait_ge(max_filled, max_no["O", o - 1] + 1)
                    nc.scalar.activation(ot[:, :], O_BANK, ACT.Copy).then_inc(o_copied, 1)

                if s in square_steps:
                    c, pair = square_steps[s]
                    wait_item(act, "WO", c, pair)
                    for i in range(2):
                        sum_squares(1, c * CT + 2 * pair + i, attn[:, c * CT + 2 * pair + i, :])
                if s in fw_loads:
                    r = fw_loads[s]
                    if r:
                        act.wait_ge(max_filled, max_no["FW", 2 * r - 1] + 1)
                    if r < 4:
                        src = (gate_w, hid_w)[r // 2][(r % 2) * 512:(r % 2 + 1) * 512, :]
                        act.dma_start(f_raw[:, :, :], src.rearrange("(t p) d -> p t d", p=P)).then_inc(f_loaded, 16)
                    else:
                        act.dma_start(f_raw[:, :, :].rearrange("p a d -> p (a d)").rearrange("p (t n) -> p t n", t=KT),
                                      out_w[:, (r - 4) * 512:(r - 3) * 512].rearrange("(t p) n -> p t n", p=P)
                                      ).then_inc(f_loaded, 16)

            def high_hidden(n):
                wait_evacuated(act, "hid", n)
                if n >= 3:
                    wait_h_used(act, n - 3)
                nc.scalar.activation(h_hi[n % 3][:, :], h_f[n % 2][:, :], ACT.Copy).then_inc(h_hi_ready, 1)

            for step in fin:
                what, rest = step[0], step[1:]
                if what == "a_T":
                    c, kt = rest
                    wait_filled(act, "a_T", c, kt)
                    nc.scalar.activation(at_hi[:, kt, :], bank_of("a_T", c, kt), ACT.Copy).then_inc(at_hi_ready, 1)
                elif what == "WO":
                    c, pair = rest
                    wait_evacuated(act, "WO", c, pair)
                    for i in range(2):
                        sum_squares(1, c * CT + 2 * pair + i, attn[:, c * CT + 2 * pair + i, :])
                elif what == "y_T":
                    norm_affine(1, *rest)
                elif what == "F":
                    n = rest[0]
                    if n < len(ffn_units):
                        wait_filled(act, "gate", n)
                        if n >= 2:
                            wait_evacuated(act, "hid", n - 2)
                        nc.scalar.activation(silu_g[n % 2][:, :], bank_of("gate", n), ACT.Silu
                                             ).then_inc(free_sem("gate", n), 1)
                    if 1 <= n <= len(ffn_units):
                        high_hidden(n - 1)

        @block.vector
        def _(dve):
            steps = [0]

            def link(ins):
                steps[0] += 1
                ins.then_inc(vector_step, 1)
                dve.wait_ge(vector_step, steps[0])

            dve.wait_ge(par_loaded, 16 * 3)
            nc.vector.tensor_copy(par_twice[:, :].rearrange("r (a c) -> r a c", a=2),
                                  par_rows[:, :].unsqueeze(1).to_broadcast([7, 2, QUAT])).then_inc(par_doubled, 1)
            wait_filled(dve, "par")
            nc.vector.tensor_copy(qc[:, 0:7], bank_of("par")[:, 0:7]).then_inc(free_sem("par"), 1)
            wait_evacuated(dve, "par")
            link(nc.vector.tensor_tensor(small[:, 0:6], qc[:, 0:6], qc[:, 0:6], ALU.mult))
            nc.vector.reduce_sum(small[:, 6:7], small[:, 0:4], AX.X)
            link(nc.vector.reduce_sum(small[:, 7:8], small[:, 4:6], AX.X))
            nc.vector.tensor_scalar_add(small[:, 6:8], small[:, 6:8], QEPS).then_inc(norms_summed, 1)
            dve.wait_ge(norms_rooted, 1)
            link(nc.vector.tensor_scalar(small[:, 12:16], qc[:, 0:4], small[:, 10:11], qc[:, 6:7], ALU.mult, ALU.mult))
            nc.vector.tensor_scalar(small[:, 16:20], small[:, 12:16], -1.0, None, ALU.mult)
            link(nc.vector.tensor_scalar(small[:, 20:22], qc[:, 4:6], small[:, 11:12], None, ALU.mult))
            right = small[:, 24:32].rearrange("p (t k) -> p t k", t=KT)
            signed = ((0, 5, 6, 7), (1, 0, 3, 6), (2, 7, 0, 1), (3, 2, 5, 0))
            for j, row in enumerate(signed):
                part = slice(QUAT * (j % 2), QUAT * (j % 2) + QUAT)
                for k, i in enumerate(row):
                    last = nc.vector.tensor_copy(right[part, j // 2, k:k + 1], small[part, 12 + i:13 + i])
            link(last)
            tmp = small[:, 32:40].rearrange("p (t k) -> p t k", t=KT)
            cross = small[:, 40:48].rearrange("p (t k) -> p t k", t=KT)

            def r(k):
                return right[:, :, k:k + 1]

            for k, (a, b, op) in enumerate(((1, 2, ALU.add), (3, 2, ALU.subtract), (1, 3, ALU.subtract),
                                            (2, 1, ALU.subtract))):
                last = nc.vector.tensor_tensor(tmp[:, :, k:k + 1], r(a), r(b), op)
            link(last)
            nc.vector.scalar_tensor_tensor(out=cross[:, :, 0:1], in0=tmp[:, :, 0:1], scalar=-1.0, in1=r(3),
                                           op0=ALU.mult, op1=ALU.subtract)
            link(nc.vector.tensor_tensor(cross[:, :, 1:4], tmp[:, :, 1:4], r(0).to_broadcast([P, KT, 3]), ALU.add))
            link(nc.vector.tensor_scalar(small[:, 48:56], small[:, 40:48], small[:, 21:22], None, ALU.mult))
            link(nc.vector.scalar_tensor_tensor(out=small[:, 56:64], in0=small[:, 24:32], scalar=small[:, 20:21],
                                                in1=small[:, 48:56], op0=ALU.mult, op1=ALU.add))
            dve.wait_ge(consts_ready, 2)
            rot_blocks = rot[:, :, :].rearrange("p t (k c) -> p (t k) c", c=QUAT)
            link(nc.vector.tensor_tensor(rot_blocks, diag64[:, :].unsqueeze(1).to_broadcast([P, 8, QUAT]),
                                         small[:, 56:64].unsqueeze(2).to_broadcast([P, 8, QUAT]), ALU.mult))
            for kt in range(KT):
                diag = rot[:, kt, kt * P:(kt + 1) * P]
                last = nc.vector.tensor_tensor(diag, diag, ident[:, :], ALU.add)
            last.then_inc(rot_ready, 1)

            wait_filled(dve, "bias")
            nc.vector.tensor_copy(qc[:, 7:15], bank_of("bias")[:, 0:8]).then_inc(free_sem("bias"), 1)
            wait_evacuated(dve, "bias")
            dve.wait_ge(cond_loaded, 16 * 5)
            for b in range(BATCH):
                link(nc.vector.tensor_tensor(gprod[:, :, :], gw[:, :, :],
                                             cond_bc[:, b:b + 1, :].to_broadcast([P, 8, DT]), ALU.mult))
                link(nc.vector.reduce_sum(gb[:, b, :], gprod[:, :, :], AX.X))
                last = nc.vector.tensor_tensor(gb[:, b, :], gb[:, b, :], qc[:, 7:15], ALU.add)
            last.then_inc(gb_ready, 1)

            def mean_squares(norm, c):
                t = slice(c * CT, (c + 1) * CT)
                nc.vector.tensor_scalar(ms[:, norm, t], sumsq[:, norm, t], 1.0 / D, NEPS, ALU.mult, ALU.add
                                        ).then_inc(ms_ready, 1)

            def scale_tokens(norm, c, src, dst, ready):
                dve.wait_ge(inv_ready, NCH * norm + c + 1)
                for i in range(CT):
                    n = c * CT + i
                    last = nc.vector.tensor_scalar(dst[:, i, :], src[:, n, :], inv_rms[:, norm, n:n + 1], None,
                                                   ALU.mult)
                last.then_inc(ready, 1)

            def split_maxima(n, step):
                all_max = nmax[:, n % 2, :, :].rearrange("p h t -> p (h t)")
                if step == 0:
                    wait_item(dve, "max", HU * n + HU - 1)
                    ins = nc.vector.tensor_copy(nmax_parts[:, 0, :], all_max)
                elif step == 1:
                    dve.wait_ge(parts_step, 3 * n + 1)
                    ins = nc.vector.tensor_tensor(nmax_rest[:, :], all_max, nmax_parts[:, 0, :], ALU.subtract)
                elif step == 2:
                    dve.wait_ge(parts_step, 3 * n + 2)
                    ins = nc.vector.tensor_copy(nmax_parts[:, 1, :], nmax_rest[:, :])
                else:
                    dve.wait_ge(parts_step, 3 * n + 3)
                    ins = nc.vector.tensor_tensor(nmax_parts[:, 2, :], nmax_rest[:, :], nmax_parts[:, 1, :],
                                                  ALU.subtract)
                ins.then_inc(nmax_split if step == 3 else parts_step, 1)

            def item_of_max_slot(item):
                what, n = item[0], item[1]
                slot = max_slot(item)
                if what == "max" and n >= HU:
                    for step in {0: (0,), 1: (1,), 2: (2, 3)}.get(n % HU, ()):
                        split_maxima(n // HU - 1, step)
                elif what == "T" and n == NG * NHALF - 1:
                    for step in range(4):
                        split_maxima(n, step)
                dve.wait_ge(max_filled, max_no[item] + 1)
                if what == "max":
                    b, h, t = n // HU % 2, n % HU // HT_Q, n % HT_Q
                    nc.vector.tensor_reduce(out=nmax[:, b, h, t:t + 1], in_=slot, axis=AX.XY, op=ALU.max,
                                            negate=True).then_inc(max_used, 1)
                elif what == "T":
                    if n:
                        dve.wait_ge(nmax_saved, 16 * n)
                    nc.vector.tensor_copy(nmax_t[:, :], slot[0:3 * HU, 0, 0:P // 2].bitcast(bf16)).then_inc(max_used, 1)
                elif what == "O":
                    o = slot[:, 0, :].rearrange("p (t h d) -> p t h d", t=CT, h=GH)
                    g, half = n // NHALF, n % NHALF
                    b, hg = g // (NG // BATCH), g % (NG // BATCH)
                    t = b * LT + half * CT
                    if n:
                        wait_item(dve, "O", n - 1)
                    link(nc.vector.reciprocal(rsum[:, :, :, :], o[:, :, :, DH:VW]))
                    nc.vector.tensor_tensor(
                        attn[:, t:t + CT, hg * GH * DH:(hg + 1) * GH * DH].rearrange("p t (h d) -> p t h d", d=DH),
                        o[:, :, :, 0:DH], rsum[:, :, :, :].to_broadcast([P, CT, GH, DH]), ALU.mult
                    ).then_inc(max_used, 1)
                elif what == "WO":
                    t = n * CT + 2 * item[2]
                    nc.vector.tensor_tensor(attn[:, t:t + 2, :], slot[:, 0, :].rearrange("p (t d) -> p t d", t=2),
                                            x1[:, t:t + 2, :], ALU.add).then_inc(max_used, 1)
                else:
                    i = cut_no[item]
                    if i >= 2:
                        wait_cut(dve, *cuts[i - 2])
                    if what == "y_T":
                        ins = nc.vector.tensor_scalar(yn_f[:, i % 2, :], slot[:, 0, :], gb_col(n // BCH, 1, 0, item[2]),
                                                      gb_col(n // BCH, 1, 1, item[2]), ALU.mult, ALU.add)
                    else:
                        ins = nc.vector.tensor_copy(yn_f[:, i % 2, :], slot[:, 0, :])
                    ins.then_inc(max_used, 1)

            for step in prep:
                what, rest = step[0], step[1:]
                if what == "W":
                    for i in range(4):
                        dve.wait_ge(w_hi_ready, i + 1)
                        hi, lo = (w_hi[:, i, :, :], w_lo[:, i, :, :]) if i < 3 else (wo_hi[:, :, :], wo_lo[:, :, :])
                        nc.vector.tensor_tensor(lo, bank_of("W", i).rearrange("p (k d) -> p k d", k=KT),
                                                hi.bitcast(f32), ALU.subtract).then_inc(free_sem("W", i), 1)
                elif what == "SC":
                    c = rest[0]
                    for pair in range(2):
                        wait_evacuated(dve, "L0", c, pair)
                    mean_squares(0, c)
                    if c < DVE_CHUNKS:
                        if c >= 2:
                            wait_filled(dve, "xs_T", c - 2, 1)
                        scale_tokens(0, c, x1, xs[c % 2], xs_ready)
                elif what == "xs_T":
                    c = rest[0]
                    if 2 <= c < DVE_CHUNKS:
                        wait_filled(dve, "V", c - 2, 1)
                    for kt in range(KT if c < DVE_CHUNKS else 0):
                        wait_evacuated(dve, "xs_T", c, kt)
                        nc.vector.tensor_copy(xn_hi[c % 2][:, kt, :], xf[:, kt, :]).then_inc(xn_hi_ready, 1)
                        dve.wait_ge(xn_hi_ready, KT * c + kt + 1)
                        nc.vector.tensor_tensor(xn_lo[c % 2][:, kt, :], xf[:, kt, :],
                                                xn_hi[c % 2][:, kt, :].bitcast(f32), ALU.subtract
                                                ).then_inc(xn_lo_ready, 1)
                elif what == "QK":
                    c, j = rest
                    n = 4 * c + j
                    dve.wait_ge(part1_ready, n + 1)
                    if n >= 3:
                        dve.wait_ge(parts_ready, n - 2)
                    nc.vector.scalar_tensor_tensor(out=qk_rest[n % 3][:, :], in0=bank_of("QK", c, j),
                                                   scalar=1.0 if j % 2 else DH ** -0.5,
                                                   in1=qk_parts[j][:, 0, :], op0=ALU.mult, op1=ALU.subtract
                                                   ).then_inc(free_sem("QK", c, j), 1)
                elif what == "item":
                    item_of_max_slot(rest[0])

            if prep_total[7]:
                dve.wait_ge(evacuated[7], prep_total[7])
            nc.vector.memset(O_BANK, 0.0).then_inc(o_cleared, 1)
            wait_preparation(dve)
            for s in range(NSTEP):
                for item in max_items(s):
                    item_of_max_slot(item)
                if s in mean_steps:
                    c = mean_steps[s]
                    dve.wait_ge(squares_done, NT + CT * (c + 1))
                    mean_squares(1, c)

            for step in fin:
                what, rest = step[0], step[1:]
                if what == "O":
                    item_of_max_slot(step)
                    continue
                if what == "a_T":
                    c, kt = rest
                    dve.wait_ge(at_hi_ready, KT * (c - BCH) + kt + 1)
                    nc.vector.tensor_tensor(at_lo[:, kt, :], bank_of("a_T", c, kt), at_hi[:, kt, :].bitcast(f32),
                                            ALU.subtract).then_inc(free_sem("a_T", c, kt), 1)
                    continue
                if what == "WO":
                    c, pair = rest
                    t = c * CT + 2 * pair
                    wait_filled(dve, "WO", c, pair)
                    nc.vector.tensor_tensor(attn[:, t:t + 2, :], bank_of("WO", c, pair).rearrange("p (t d) -> p t d", t=2),
                                            x1[:, t:t + 2, :], ALU.add).then_inc(free_sem("WO", c, pair), 1)
                    continue
                if what == "SC":
                    c = rest[0]
                    dve.wait_ge(squares_done, NT + CT * (c + 1))
                    mean_squares(1, c)
                    scale_tokens(1, c, attn, xs2, ys_ready)
                    continue
                if what == "y_T":
                    c, kt = rest
                    wait_evacuated(dve, "y_T", c, kt)
                    nc.vector.tensor_copy(yn_hi[c][:, kt, :], yn_f[:, kt, :]).then_inc(yn_hi_ready, 1)
                    continue
                n = rest[0]
                if n < len(ffn_units):
                    wait_evacuated(dve, "gate", n)
                    wait_filled(dve, "hid", n)
                    if n >= 2:
                        dve.wait_ge(h_lo_ready, n - 1)
                    nc.vector.tensor_tensor(h_f[n % 2][:, :], bank_of("hid", n), silu_g[n % 2][:, :], ALU.mult
                                            ).then_inc(free_sem("hid", n), 1)
                if n >= OUT_LAG and ffn_units[n - OUT_LAG][1] == HT - 1:
                    c = ffn_units[n - OUT_LAG][0]
                    dve.wait_ge(x12_ready, c + 1)
                    for tt in range(CT):
                        wait_filled(dve, "out", c, tt)
                        nc.vector.tensor_tensor(attn[:, c * CT + tt, :], bank_of("out", c, tt)[:, 0:D],
                                                x1[:, c * CT + tt, :], ALU.add).then_inc(free_sem("out", c, tt), 1)

        @block.tensor
        def _(pe):
            def blocks(dst, srcs):
                for i, src in enumerate(srcs):
                    last = nc.tensor.transpose(dst[:, i * P:(i + 1) * P], src, ident[:, :])
                return last

            def transposes(key, srcs):
                wait_bank(pe, *key)
                blocks(bank_of(*key), srcs).then_inc(tile_filled, 1)

            def a_blocks(c, kt):
                return [attn[:, c * CT + t, kt * P:(kt + 1) * P] for t in range(CT)]

            def y_blocks(kt):
                return [xs2[:, t, kt * P:(kt + 1) * P] for t in range(CT)]

            def project_out(dst, pair):
                for i in range(2):
                    t = slice((2 * pair + i) * P, (2 * pair + i + 1) * P)
                    last = split_product(dst[:, i * D:(i + 1) * D],
                                         [(at_hi[:, kt, t], at_lo[:, kt, t]) for kt in range(KT)],
                                         [(wo_hi[:, kt, :], wo_lo[:, kt, :]) for kt in range(KT)])
                return last

            def split_product(dst, stationary, moving, first=True, last=True):
                passes = [(s, m) for (sh, sl), (mh, ml) in zip(stationary, moving)
                          for s, m in ((sl, mh), (sh, ml), (sh, mh))]
                for i, (s, m) in enumerate(passes):
                    ins = nc.tensor.matmul(dst, s, m, start=first and i == 0, stop=last and i == len(passes) - 1)
                return ins

            pe.wait_ge(consts_ready, 1)
            pe.wait_ge(par_doubled, 1)
            nc.tensor.transpose(bank_of("par")[:, 0:7], par_twice[:, :], ident[0:7, 0:7]).then_inc(tile_filled, 1)

            def qkv_ready(c):
                if c == 0:
                    for i in range(3):
                        wait_evacuated(pe, "W", i)
                for kt in range(KT):
                    wait_evacuated(pe, "xs_T", c, kt)
                pe.wait_ge(xn_lo_ready, KT * (c + 1))

            def operands_loaded(g):
                pe.wait_ge(stack_loaded[g % SLOTS], 16 * 2 * len(K_PARTS) * (g // SLOTS + 1))

            def do_item(item):
                what, n = item[0], item[1]
                slot = max_slot(item)
                if max_no[item] >= 2:
                    pe.wait_ge(max_used, max_no[item] - 1)
                else:
                    for i in range(4):
                        pe.wait_ge(evacuated[i], before_items[i])
                    pe.wait_ge(consts_ready, 3)
                if what == "max":
                    g, h, lt = unit(n)
                    if n % GU == 0:
                        operands_loaded(g)
                    for half in range(SEQ // 512):
                        last = nc.tensor.matmul(slot[:, half, :], q_st[g % SLOTS][0:PROD_ROWS, h, lt * P:(lt + 1) * P],
                                                k_st[g % SLOTS][0:PROD_ROWS, h, half * 512:(half + 1) * 512],
                                                start=True, stop=True)
                elif what == "T":
                    pe.wait_ge(nmax_split, n + 1)
                    last = nc.tensor.transpose(slot[0:3 * HU, 0, 0:P // 2].bitcast(bf16),
                                               nmax_parts[:, :, :].rearrange("p a q -> p (a q)"), ident_bf[:, :])
                elif what == "O":
                    pe.wait_ge(o_copied, n + 1)
                    last = blocks(slot[:, 0, :], [ot[:, t * P:(t + 1) * P] for t in range(CT)])
                elif what == "a_T":
                    last = blocks(slot[:, 0, :], a_blocks(n, item[2]))
                elif what == "WO":
                    wait_cut(pe, "a_T", n, 1)
                    last = project_out(slot[:, 0, :], item[2])
                elif what == "y_T":
                    pe.wait_ge(ys_ready, n + 1)
                    last = blocks(slot[:, 0, :], y_blocks(item[2]))
                else:
                    r, i = n // 2, n % 2
                    pe.wait_ge(f_loaded, 16 * (r + 1))
                    if r < 4:
                        srcs = [f_raw[:, t, i * P:(i + 1) * P] for t in range(CT)]
                    else:
                        raw = f_raw[:, :, :].rearrange("p a d -> p (a d)").rearrange("p (t n) -> p t n", t=KT)
                        srcs = [raw[:, t, (2 * i + a) * P:(2 * i + a + 1) * P] for a in range(2) for t in range(KT)]
                    last = blocks(slot[:, 0, :], srcs)
                last.then_inc(max_filled, 1)

            def scores(s, h):
                g, half, kt = s // (NHALF * LT), s // LT % NHALF, s % LT
                e = GH * s + h
                if e >= EB:
                    pe.wait_ge(exp_done, e - EB + 1)
                if s % LT == 0 and h == 0:
                    pe.wait_ge(max_loaded[NHALF * (g % SLOTS) + half], 16 * (g // SLOTS + 1))
                nc.tensor.matmul(e_bank(e), k_st[g % SLOTS][0:ALL_ROWS, h, kt * P:(kt + 1) * P],
                                 q_st[g % SLOTS][0:ALL_ROWS, h, half * HALF:(half + 1) * HALF],
                                 start=True, stop=True).then_inc(scores_filled, 1)

            def values(s):
                g, kt = s // (NHALF * LT), s % LT
                b, hg = g // (NG // BATCH), g % (NG // BATCH)
                pe.wait_ge(exp_done, GH * (s + 1))
                if kt == 0:
                    if s:
                        pe.wait_ge(o_copied, s // LT)
                    else:
                        pe.wait_ge(o_cleared, 1)
                for h in range(GH):
                    last = nc.tensor.matmul(O_BANK[32 * h:32 * h + VW, :], v_sb[:, b * LT + kt, hg * GH + h, :],
                                            prob[(GH * s + h) % PR][:, :], start=kt == 0, stop=kt == LT - 1)
                last.then_inc(pv_done, 1)

            for step in prep:
                what, rest = step[0], step[1:]
                if what == "x_T":
                    c = rest[0]
                    pe.wait_ge(x_loaded[c], 16)
                    for kt in range(KT):
                        transposes(("x_T", c, kt), [x_in[c % 2][:, t, kt * P:(kt + 1) * P] for t in range(CT)])
                elif what == "bias":
                    pe.wait_ge(bias_loaded, 16 * 4)
                    wait_bank(pe, "bias")
                    nc.tensor.transpose(bank_of("bias")[:, 0:8], bias_rows[:, :], ident[0:8, 0:8]
                                        ).then_inc(tile_filled, 1)
                elif what == "W":
                    pe.wait_ge(w_loaded, 16 * 4)
                    for i in range(4):
                        transposes(("W", i), [w_raw[:, i, t, kt * P:(kt + 1) * P]
                                              for kt in range(KT) for t in range(KT)])
                elif what == "L0":
                    c = rest[0]
                    if c == 0:
                        pe.wait_ge(rot_ready, 1)
                    for kt in range(KT):
                        wait_evacuated(pe, "x_T", c, kt)
                    for pair in range(2):
                        wait_bank(pe, "L0", c, pair)
                        for i in range(2):
                            t = 2 * pair + i
                            for kt in range(KT):
                                last = nc.tensor.matmul(bank_of("L0", c, pair)[:, i * D:(i + 1) * D],
                                                        x_t[c % 2][:, kt, t * P:(t + 1) * P], rot[:, kt, :],
                                                        start=kt == 0, stop=kt == KT - 1)
                        last.then_inc(tile_filled, 1)
                elif what == "xs_T":
                    c = rest[0]
                    pe.wait_ge(xs_ready, c + 1)
                    for kt in range(KT):
                        transposes(("xs_T", c, kt), [xs[c % 2][:, t, kt * P:(kt + 1) * P] for t in range(CT)])
                elif what == "QK":
                    c, j = rest
                    if j == 0:
                        qkv_ready(c)
                    hi, lo = xn_hi[c % 2], xn_lo[c % 2]
                    cols = slice((j // 2) * P, (j // 2 + 1) * P)
                    wait_bank(pe, "QK", c, j)
                    split_product(bank_of("QK", c, j),
                                  [(w_hi[:, j % 2, kt, cols], w_lo[:, j % 2, kt, cols]) for kt in range(KT)],
                                  [(hi[:, kt, :], lo[:, kt, :]) for kt in range(KT)]).then_inc(tile_filled, 1)
                elif what == "V":
                    c, pair = rest
                    hi, lo = xn_hi[c % 2], xn_lo[c % 2]
                    wait_bank(pe, "V", c, pair)
                    for i in range(2):
                        t = slice((2 * pair + i) * P, (2 * pair + i + 1) * P)
                        last = split_product(bank_of("V", c, pair)[:, i * D:(i + 1) * D],
                                             [(hi[:, kt, t], lo[:, kt, t]) for kt in range(KT)],
                                             [(w_hi[:, 2, kt, :], w_lo[:, 2, kt, :]) for kt in range(KT)])
                    last.then_inc(tile_filled, 1)
                elif what == "item":
                    do_item(rest[0])

            for i in range(4, 8):
                pe.wait_ge(evacuated[i], prep_total[i])
            pe.wait_ge(ones_loaded, 16 * SLOTS)
            for s in range(NSTEP + 1):
                if s < NSTEP:
                    for h in range(GH - 1):
                        scores(s, h)
                items = max_items(s) if s < NSTEP else []
                early = 1 if items and items[0][0] == "max" else 0
                for item in items[:early]:
                    do_item(item)
                if 1 <= s <= NSTEP:
                    values(s - 1)
                if s < NSTEP:
                    scores(s, GH - 1)
                for item in items[early:]:
                    do_item(item)

            pe.wait_ge(exp_done, GH * NSTEP)
            for step in fin:
                what, rest = step[0], step[1:]
                if what == "a_T":
                    transposes(("a_T", *rest), a_blocks(*rest))
                    continue
                if what == "WO":
                    c, pair = rest
                    for kt in range(KT):
                        wait_evacuated(pe, "a_T", c, kt)
                    wait_bank(pe, "WO", c, pair)
                    project_out(bank_of("WO", c, pair), pair).then_inc(tile_filled, 1)
                    continue
                if what == "y_T":
                    c, kt = rest
                    pe.wait_ge(ys_ready, c + 1)
                    transposes(("y_T", c, kt), y_blocks(kt))
                    continue
                if what == "O":
                    do_item(step)
                if what != "F":
                    continue
                n = rest[0]
                if n == OUT_LAG:
                    pe.wait_ge(max_used, len(max_no))
                if n < len(ffn_units):
                    c, ht = ffn_units[n]
                    if n == 0:
                        pe.wait_ge(cut_ready, len(cuts))
                    if ht == 0 and c >= BCH:
                        pe.wait_ge(yn_lo_ready, KT * (c - BCH + 1))
                    cols = slice(ht * P, (ht + 1) * P)
                    for w, name in enumerate(("gate", "hid")):
                        wait_bank(pe, name, n)
                        split_product(bank_of(name, n),
                                      [(fw_hi[:, w, kt, cols], fw_lo[:, w, kt, cols]) for kt in range(KT)],
                                      [(yn_hi[c][:, kt, :], yn_lo[c][:, kt, :]) for kt in range(KT)]
                                      ).then_inc(tile_filled, 1)
                if n >= OUT_LAG:
                    m = n - OUT_LAG
                    c, ht = ffn_units[m]
                    pe.wait_ge(h_lo_ready, m + 1)
                    for tt in range(CT):
                        if ht == 0:
                            wait_bank(pe, "out", c, tt)
                        t = slice(tt * P, (tt + 1) * P)
                        ins = split_product(bank_of("out", c, tt)[:, 0:D], [(h_hi[m % 3][:, t], h_lo[m % 3][:, t])],
                                            [(fo_hi[:, ht, :], fo_lo[:, ht, :])], ht == 0, ht == HT - 1)
                        if ht == HT - 1:
                            ins.then_inc(tile_filled, 1)
                    if ht < HT - 1:
                        ins.then_inc(h_used, 1)


NAMES = ["x", "cond_256", "L0_cond_q_right", "L0_cond_spectral_gate", "L1_cond_Wq", "L1_cond_Wk", "L1_cond_Wv",
         "L1_cond_Wo", "L1_cond_g1w", "L1_cond_g1b", "L1_cond_b1w", "L1_cond_b1b", "L1_cond_g2w", "L1_cond_g2b",
         "L1_cond_b2w", "L1_cond_b2b", "L1_cond_gate_w", "L1_cond_hid_w", "L1_cond_out_w"]


def kernel(**inputs):
    import numpy as _np
    import concourse.bacc as _bacc
    from concourse import mybir as _mybir
    from concourse.bass_utils import run_bass_kernel_spmd as _run

    nc = _bacc.Bacc("TRN2", target_bir_lowering=False, num_devices=1)
    arrays, args = {}, []
    for name in NAMES:
        a = _np.ascontiguousarray(inputs[name])
        arrays[f"in_{name}"] = a
        args.append(nc.dram_tensor(f"in_{name}", a.shape, _mybir.dt.from_np(a.dtype), kind="ExternalInput").ap())
    args.append(nc.dram_tensor("out_x", (BATCH, SEQ, D), _mybir.dt.float32, kind="ExternalOutput").ap())
    build(nc, *args)
    r = _run(nc, [arrays], core_ids=[0])
    return r.results[0]["out_x"]
```
